# Optimizing a Trainium2 kernel written in Bass

```python
import numpy as np
import jax
import jax.numpy as jnp

def _softmax(x, axis=-1):
    return jax.nn.softmax(x, axis=axis)

def _gelu(x):
    return jax.nn.gelu(x, approximate=True)

def _silu(x):
    return jax.nn.silu(x)

def _sigmoid(x):
    return jax.nn.sigmoid(x)

def _layernorm(x, axis=-1, eps=1e-05):
    m = jnp.mean(x, axis=axis, keepdims=True)
    v = jnp.var(x, axis=axis, keepdims=True)
    return (x - m) / jnp.sqrt(v + eps)

def _scatter_add(tgt, idx, src, axis=0):
    return tgt.at[idx].add(src)

def _segment_sum(src, seg, n):
    return jax.ops.segment_sum(src, seg, n)
kernel_name = 'mk_flamingo_gated_d2_seqx_r8_06e8e5'

def setup_inputs(seed: int=0):
    np.random.seed(seed)
    _w = jnp.asarray

    def _rec_inputs():
        import jax
        import jax.numpy as jnp
        _rk = jax.random.key(seed)
        x = -0.0002928 + 1 * jax.random.normal(jax.random.fold_in(_rk, 1), (32, 128, 128), jnp.float32)
        _lenS = 128 - jax.random.randint(jax.random.fold_in(_rk, 7), (32,), 0, max(1, 128 // 4) + 1, jnp.int32)
        _lenS2 = 128 - jax.random.randint(jax.random.fold_in(_rk, 8), (32,), 0, max(1, 128 // 4) + 1, jnp.int32)
        _ctx_1024P = jax.random.normal(jax.random.fold_in(_rk, 11), (32, 16, 128), jnp.float32)
        _ctx_1024c = jax.random.dirichlet(jax.random.fold_in(_rk, 511), 0.3 * jnp.ones((16,), jnp.float32), (32, 128))
        _ctx_1024t = jnp.einsum('bsk,bkd->bsd', _ctx_1024c, _ctx_1024P)
        _ctx_1024t = _ctx_1024t * jax.lax.rsqrt(jnp.mean(jnp.square(_ctx_1024t)) + 1e-12) * 0.953939
        ctx_1024 = -1.39393e-06 + 0.999914 * (_ctx_1024t + 0.3 * jax.random.normal(jax.random.fold_in(_rk, 611), (32, 128, 128), jnp.float32))
        _g = jax.random.normal(jax.random.fold_in(_rk, 9001), (2, 2), jnp.float32)
        _g = jnp.sign(_g) * jnp.maximum(jnp.abs(_g), 1.0) + (_g == 0) * 1.0
        g_xattn = _g[0]
        g_ffn = _g[1]
        return (x, ctx_1024, g_xattn, g_ffn)
    x, ctx_1024, g_xattn, g_ffn = _rec_inputs()

    def _L0_xattn_setup():
        import jax, jax.numpy as jnp
        import numpy as np
        D_MODEL = 128
        NUM_HEADS = 16
        HEAD_DIM = D_MODEL // NUM_HEADS
        key = jax.random.key(seed)
        ks = jax.random.split(key, 11)
        B, S, D = (2, 256, D_MODEL)
        s = 1.0 / np.sqrt(D)
        inp = {'query': jax.random.normal(ks[0], (B, S, D), jnp.float32), 'key': jax.random.normal(ks[1], (B, S, D), jnp.float32), 'value': jax.random.normal(ks[2], (B, S, D), jnp.float32), 'Wq': jax.random.normal(ks[3], (D, D), jnp.float32) * s, 'bq': jnp.zeros((D,), jnp.float32), 'Wk': jax.random.normal(ks[4], (D, D), jnp.float32) * s, 'bk': jnp.zeros((D,), jnp.float32), 'Wv': jax.random.normal(ks[5], (D, D), jnp.float32) * s, 'bv': jnp.zeros((D,), jnp.float32), 'Wo': jax.random.normal(ks[6], (D, D), jnp.float32) * s, 'bo': jnp.zeros((D,), jnp.float32)}
        return inp
    _L0_xattn_all = _L0_xattn_setup()
    _L0_xattn_in = {k: v for k, v in _L0_xattn_all.items() if k in ('Wq', 'bq', 'Wk', 'bk', 'Wv', 'bv', 'Wo', 'bo')}
    del _L0_xattn_all

    def _L0_ffn_setup():
        import jax, jax.numpy as jnp
        import numpy as np
        key = jax.random.key(seed)
        k0, k1, k2, k3 = jax.random.split(key, 4)
        B, S, D, F, E = (8, 256, 128, 256, 8)
        x = jax.random.normal(k0, (B, S, D), dtype=jnp.float32)
        Wg = jax.random.normal(k1, (D, E), dtype=jnp.float32) * 0.02
        W1 = jax.random.normal(k2, (E, D, F), dtype=jnp.float32) * 0.02
        W2 = jax.random.normal(k3, (E, F, D), dtype=jnp.float32) * 0.02
        return {'x': x, 'Wg': Wg, 'W1': W1, 'W2': W2}
    _L0_ffn_all = _L0_ffn_setup()
    _L0_ffn_in = {k: v for k, v in _L0_ffn_all.items() if k in ('Wg', 'W1', 'W2')}
    del _L0_ffn_all

    def _L1_xattn_setup():
        import jax, jax.numpy as jnp
        import numpy as np
        HEADS = 16
        key = jax.random.key(seed)
        k1, k2, k3, k4 = jax.random.split(key, 4)
        B, N, M, D = (2, 256, 256, 128)
        x = jax.random.normal(k1, (B, N, D), dtype=jnp.float32)
        context = jax.random.normal(k2, (B, M, D), dtype=jnp.float32)
        Wq = jax.random.normal(k3, (D, D), dtype=jnp.float32) * D ** (-0.5)
        Wkv = jax.random.normal(k4, (D, 2 * D), dtype=jnp.float32) * D ** (-0.5)
        return {'x': x, 'context': context, 'Wq': Wq, 'Wkv': Wkv}
    _L1_xattn_all = _L1_xattn_setup()
    _L1_xattn_in = {k: v for k, v in _L1_xattn_all.items() if k in ('Wq', 'Wkv')}
    del _L1_xattn_all

    def _L1_ffn_setup():
        import jax, jax.numpy as jnp
        import numpy as np
        EMBED_DIM = 128
        HIDDEN_DIM = 512
        NUM_EXPERTS = 8
        TOP_K = 2
        key = jax.random.key(seed)
        k_x, k_g, k_w1, k_w2 = jax.random.split(key, 4)
        x = jax.random.normal(k_x, (2, 64, EMBED_DIM), dtype=jnp.float32)
        gate_w = jax.random.normal(k_g, (NUM_EXPERTS, EMBED_DIM), dtype=jnp.float32) * (1.0 / np.sqrt(EMBED_DIM))
        w1 = jax.random.normal(k_w1, (NUM_EXPERTS, EMBED_DIM, HIDDEN_DIM), dtype=jnp.float32) * np.sqrt(2.0 / EMBED_DIM)
        b1 = jnp.zeros((NUM_EXPERTS, HIDDEN_DIM), dtype=jnp.float32)
        w2 = jax.random.normal(k_w2, (NUM_EXPERTS, HIDDEN_DIM, EMBED_DIM), dtype=jnp.float32) * np.sqrt(2.0 / HIDDEN_DIM)
        b2 = jnp.zeros((NUM_EXPERTS, EMBED_DIM), dtype=jnp.float32)
        return {'x': x, 'gate_w': gate_w, 'w1': w1, 'b1': b1, 'w2': w2, 'b2': b2}
    _L1_ffn_all = _L1_ffn_setup()
    _L1_ffn_in = {k: v for k, v in _L1_ffn_all.items() if k in ('gate_w', 'w1', 'b1', 'w2', 'b2')}
    del _L1_ffn_all
    return {'x': x, 'ctx_1024': ctx_1024, 'g_xattn': g_xattn, 'g_ffn': g_ffn, 'L0_xattn_Wq': _L0_xattn_in['Wq'], 'L0_xattn_bq': _L0_xattn_in['bq'], 'L0_xattn_Wk': _L0_xattn_in['Wk'], 'L0_xattn_bk': _L0_xattn_in['bk'], 'L0_xattn_Wv': _L0_xattn_in['Wv'], 'L0_xattn_bv': _L0_xattn_in['bv'], 'L0_xattn_Wo': _L0_xattn_in['Wo'], 'L0_xattn_bo': _L0_xattn_in['bo'], 'L0_ffn_Wg': _L0_ffn_in['Wg'], 'L0_ffn_W1': _L0_ffn_in['W1'], 'L0_ffn_W2': _L0_ffn_in['W2'], 'L1_xattn_Wq': _L1_xattn_in['Wq'], 'L1_xattn_Wkv': _L1_xattn_in['Wkv'], 'L1_ffn_gate_w': _L1_ffn_in['gate_w'], 'L1_ffn_w1': _L1_ffn_in['w1'], 'L1_ffn_b1': _L1_ffn_in['b1'], 'L1_ffn_w2': _L1_ffn_in['w2'], 'L1_ffn_b2': _L1_ffn_in['b2']}

def reference(x, ctx_1024, g_xattn, g_ffn, L0_xattn_Wq, L0_xattn_bq, L0_xattn_Wk, L0_xattn_bk, L0_xattn_Wv, L0_xattn_bv, L0_xattn_Wo, L0_xattn_bo, L0_ffn_Wg, L0_ffn_W1, L0_ffn_W2, L1_xattn_Wq, L1_xattn_Wkv, L1_ffn_gate_w, L1_ffn_w1, L1_ffn_b1, L1_ffn_w2, L1_ffn_b2):
    import jax
    import jax.numpy as jnp

    def _L0_xattn_ref(query, key, value, Wq, bq, Wk, bk, Wv, bv, Wo, bo):
        import jax, jax.numpy as jnp
        import numpy as np
        D_MODEL = 128
        NUM_HEADS = 16
        HEAD_DIM = D_MODEL // NUM_HEADS
        B, S, D = query.shape
        H, Hd = (NUM_HEADS, HEAD_DIM)
        Q = (query @ Wq.T + bq).reshape(B, S, H, Hd).transpose(0, 2, 1, 3)
        K = (key @ Wk.T + bk).reshape(B, S, H, Hd).transpose(0, 2, 1, 3)
        V = (value @ Wv.T + bv).reshape(B, S, H, Hd).transpose(0, 2, 1, 3)
        scale = 1.0 / jnp.sqrt(jnp.asarray(Hd, Q.dtype))
        scores = jnp.einsum('bhqd,bhkd->bhqk', Q, K) * scale
        attn = jax.nn.softmax(scores, axis=-1)
        out = jnp.einsum('bhqk,bhkd->bhqd', attn, V)
        out = out.transpose(0, 2, 1, 3).reshape(B, S, D)
        return out @ Wo.T + bo

    def _L0_ffn_ref(x, Wg, W1, W2):
        import jax, jax.numpy as jnp
        import numpy as np
        B, S, D = x.shape
        E = Wg.shape[1]
        T = B * S
        cap = max(1, T // E)
        xt = x.reshape(T, D)
        logits = xt @ Wg
        probs = jax.nn.softmax(logits, axis=-1)
        pT = probs.T
        _, top_idx = jax.lax.top_k(pT, cap)
        sel = jnp.zeros((E, T), dtype=bool).at[jnp.arange(E)[:, None], top_idx].set(True)
        masked = jnp.where(sel, pT, -jnp.inf)
        assigned = sel.any(axis=0)
        tok2exp = jnp.where(assigned, jnp.argmax(masked, axis=0), jnp.argmax(pT, axis=0))
        weights = jnp.take_along_axis(probs, tok2exp[:, None], axis=1)[:, 0]
        out = jnp.zeros_like(xt)
        for e in range(E):
            gate = jnp.where(tok2exp == e, weights, 0.0)
            h = jax.nn.gelu(xt @ W1[e], approximate=False) @ W2[e]
            out = out + gate[:, None] * h
        return out.reshape(B, S, D)

    def _L1_xattn_ref(x, context, Wq, Wkv):
        import jax, jax.numpy as jnp
        import numpy as np
        HEADS = 16
        B, N, D = x.shape
        M = context.shape[1]
        H = HEADS
        d = D // H
        q = (x @ Wq).reshape(B, N, H, d)
        kv = context @ Wkv
        k, v = jnp.split(kv, 2, axis=-1)
        k = k.reshape(B, M, H, d)
        v = v.reshape(B, M, H, d)
        scale = D ** (-0.5)
        sim = jnp.einsum('bihd,bjhd->bhij', q, k) * scale
        attn = jax.nn.softmax(sim, axis=-1)
        out = jnp.einsum('bhij,bjhd->bihd', attn, v)
        return out.reshape(B, N, D)

    def _L1_ffn_ref(x, gate_w, w1, b1, w2, b2):
        import jax, jax.numpy as jnp
        import numpy as np
        EMBED_DIM = 128
        HIDDEN_DIM = 512
        NUM_EXPERTS = 8
        TOP_K = 2
        orig_shape = x.shape
        xt = x.reshape(-1, EMBED_DIM)
        logits = xt @ gate_w.T
        probs = jax.nn.softmax(logits, axis=-1)
        top_w, top_i = jax.lax.top_k(probs, TOP_K)
        top_w = top_w / (top_w.sum(axis=-1, keepdims=True) + 1e-09)
        h = jnp.einsum('td,ndh->tnh', xt, w1) + b1
        h = jax.nn.gelu(h, approximate=False)
        out_all = jnp.einsum('tnh,nhd->tnd', h, w2) + b2
        sel = jnp.take_along_axis(out_all, top_i[:, :, None], axis=1)
        out = (sel * top_w[:, :, None]).sum(axis=1)
        return out.reshape(orig_shape)
    x = x + jnp.tanh(g_xattn[0]) * _L0_xattn_ref(_layernorm(x, axis=-1), ctx_1024, ctx_1024, L0_xattn_Wq, L0_xattn_bq, L0_xattn_Wk, L0_xattn_bk, L0_xattn_Wv, L0_xattn_bv, L0_xattn_Wo, L0_xattn_bo)
    x = x + jnp.tanh(g_ffn[0]) * _L0_ffn_ref(_layernorm(x, axis=-1), L0_ffn_Wg, L0_ffn_W1, L0_ffn_W2)
    x = x + jnp.tanh(g_xattn[1]) * _L1_xattn_ref(_layernorm(x, axis=-1), ctx_1024, L1_xattn_Wq, L1_xattn_Wkv)
    x = x + jnp.tanh(g_ffn[1]) * _L1_ffn_ref(_layernorm(x, axis=-1), L1_ffn_gate_w, L1_ffn_w1, L1_ffn_b1, L1_ffn_w2, L1_ffn_b2)
    return x

_drawn_inputs = setup_inputs


def setup_inputs(seed=0):
    import zlib

    import numpy as np

    out = dict(_drawn_inputs(seed))
    spreads = {'g_ffn': (-1.0, 0.2),
     'L0_xattn_bq': (0.0, 0.1),
     'L0_xattn_bk': (0.0, 0.1),
     'L0_xattn_bv': (0.0, 0.1),
     'L0_xattn_bo': (0.0, 0.1),
     'L1_ffn_b1': (0.0, 0.1),
     'L1_ffn_b2': (0.0, 0.1)}
    factors = {}
    for name, (base, spread) in spreads.items():
        noise = np.random.default_rng([zlib.crc32(name.encode()), seed]).standard_normal(out[name].shape)
        drawn = base * np.exp(spread * noise) if base else spread * noise
        out[name] = jnp.asarray(drawn.astype(out[name].dtype))
    for name, factor in factors.items():
        out[name] = (out[name] * factor).astype(out[name].dtype)
    return out
```

```python
from contextlib import ExitStack

import numpy as np

import concourse.bass as bass
from concourse import mybir

F32 = mybir.dt.float32
F16 = mybir.dt.float16
BF16 = mybir.dt.bfloat16
I32 = mybir.dt.int32
ALU = mybir.AluOpType
ACT = mybir.ActivationFunctionType
AX_X = mybir.AxisListType.X

P = 128
B = 32
D = 128
H = 16
HD = D // H
G = 4
J = 4
E = 8
T = B * P
PAIRS = B // 2
CAP = T // E
HID = (256, 512)
TILE = 256
TILES = (T // TILE + E, 2 * T // TILE + E)
REG = T + TILE
ROW = D + 2
PAD_ROW = 2 * T
LN_EPS = 1e-5
SHIFT = 16384.0
SCALE = (HD ** -0.5, D ** -0.5)
WCOLS = (2 * HID[0], 2 * HID[1] + HID[1] // P + D)
TOP_BIT = 29


def constants():
    p = np.arange(P)[:, None]
    q = np.arange(P)[None, :]
    one = np.ones((P, 1))
    parts = [
        ("ident", p == q),
        ("before", p < q),
        ("ones", np.ones((P, P))),
        ("segment", one * (np.arange(E * B)[None, :] % B != 0)),
        ("expert_less_e", one * (np.arange(E)[None, :] - E)),
        ("expert_region", one * (np.arange(E)[None, :] * REG)),
        ("tile_steps", one * (np.arange(2 * E)[None, :] * TILE)),
        ("tile_index", one * np.arange(max(TILES))[None, :]),
        ("segment8", one * (np.arange(E)[None, :] >= 0)),
        ("heads", (p % 32) // HD == np.arange(J)[None, :]),
    ]
    at, cols = {}, []
    n = 0
    for name, a in parts:
        a = np.asarray(a, np.float32) * np.ones((P, 1), np.float32)
        at[name] = (n, n + a.shape[1])
        n += a.shape[1]
        cols.append(a)
    tokens = (np.arange(B)[None, :] * P + p).astype(np.int32)
    rows = np.concatenate([tokens, tokens + T], axis=1).astype(np.int32)
    pads = np.zeros((2 * E * TILE, ROW), np.float32)
    pads[:, D] = (PAD_ROW + np.arange(2 * E * TILE)).astype(np.int32).view(np.float32)
    sel = np.zeros((P, 2, 2, G, 3, 32), np.float32)
    for k, parts_of in enumerate(((0, 0, 1), (0, 1, 0))):
        for s, part in enumerate(parts_of):
            for g in range(G):
                sel[32 * g + np.arange(32), k, part, g, s, np.arange(32)] = 1
    return at, np.concatenate(cols, axis=1), sel.reshape(P, -1), rows, pads


class Chain:

    def __init__(self, engine, sem):
        self.engine, self.sem, self.before, self.n = engine, sem, 0, 0

    def link(self, instruction):
        instruction.then_inc(self.sem, 1)
        self.n += 1
        self.engine.wait_ge(self.sem, self.before + self.n)


class Pair:

    def __init__(self, layer, half, u):
        self.u, self.n = u, half + (PAIRS // 2) * layer
        self.p = half * 2 + u
        self.g = self.n * 2 + u
        self.b = self.p * 2


class Tile:

    def __init__(self, layer, quarter, r):
        self.layer, self.r, self.u = layer, r, r % 2
        self.n = quarter + (TILES[0] // 4) * layer
        self.i = quarter * 4 + r
        self.g = self.n * 4 + r
        self.h = self.n * 2 + r // 2
        self.banks = 1 + layer
        self.hb = self.i * self.banks + TILES[0] * layer


def program(nc, at, x_in, ctx_in, gates_in, wsq_in, wg_in, vec_in, w0_in, w1_in, const_in,
            sel_in, rows_in, pads_in, out):
    xs = [nc.dram_tensor(f"dispatched{k}", [E * REG + E * TILE, ROW], F32, kind="Internal").ap() for k in (0, 1)]
    ys = [nc.dram_tensor(f"returned{k}", [PAD_ROW + 2 * E * TILE, D], F32, kind="Internal").ap() for k in (0, 1)]

    with ExitStack() as ctx:
        ctx.enter_context(nc.allow_low_precision(reason="counts up to 32 are exact in bfloat16"))

        def sb(name, shape, dt=F32):
            return ctx.enter_context(nc.sbuf_tensor(name, shape, dt))

        X = sb("X", [P, T])
        N = sb("N", [P, B, ROW])
        N2 = sb("N2", [P, B, ROW])
        CONST = sb("CONST", [P, const_in.shape[1]])
        GATES = sb("GATES", [P, 4])
        WSQ = sb("WSQ", [P, 7, D])
        WG = sb("WG", [P, 2, E])
        VEC = sb("VEC", [P, 2 * D + 4])
        LG = sb("LG", [P, B * E])
        BEFORE = sb("BEFORE", [P, P], BF16)
        ONES = sb("ONES", [P, P], BF16)
        ROWS = sb("ROWS", [P, 2 * B], I32)
        WALL = sb("WALL", [P, E * max(WCOLS)])
        CX = sb("CX", [P, 2, 2 * D])
        STATS = sb("STATS", [P, 2, 6])
        MV = sb("MV", [P, 2, 2, 2])
        EXPO = sb("EXPO", [P, 2])
        VE = sb("VE", [P, 2])
        RSTD = sb("RSTD", [P, 2, 2])
        STATS_N = sb("STATS_N", [P, 2, 6])
        MV_N = sb("MV_N", [P, 2, 2, 2])
        VE_N = sb("VE_N", [P, 2])
        RSTD_N = sb("RSTD_N", [P, 2, 2])
        XN = sb("XN", [P, 2, 2 * D])
        XN_N = sb("XN_N", [P, 2, 2 * D])
        XT = sb("XT", [P, 2, 4 * D])
        HL = sb("HL", [P, 2, 2, 4 * D], F16)
        SEL = sb("SEL", [P, 4, G, 96], F16)
        QL = sb("QL", [96, G, 2 * P], F16)
        QS = sb("QS", [P, 2, 2, H, P], F16)
        KS = sb("KS", [P, 2, G, 2 * P], F16)
        VA = sb("VA", [P, 2, 2, H, 32])
        MX = sb("MX", [P, 2, 32])
        MH = sb("MH", [32, 2, 2, P], F16)
        PT = sb("PT", [P, 2, H, P])
        OT = sb("OT", [P, 2, 4 * P])
        RC = sb("RC", [P, 2, H])
        OK = sb("OK", [P, 2 * D])
        OKT = sb("OKT", [P, 2 * D])
        NT = sb("NT", [P, 2 * D])
        PR = sb("PR", [P, B, E])
        RA = sb("RA", [P, E, B])
        RB = sb("RB", [P, E, B])
        RK = sb("RK", [P, E, B])
        OH = sb("OH", [P, E, B])
        MASK = sb("MASK", [P, E, B], BF16)
        SM = sb("SM", [P, 8, B])
        CN = sb("CN", [P, E], BF16)
        EX = sb("EX", [P, 8, E])
        IV = sb("IV", [P, 4, E], I32)
        BITF = sb("BITF", [P, 1])
        SLOT = sb("SLOT", [P, 2, B], I32)
        NTM = max(TILES)
        TT = sb("TT", [P, 3, NTM, E])
        TV = sb("TV", [P, 4, NTM])
        TBL = sb("TBL", [P, 2, NTM], I32)
        CNTI = sb("CNTI", [P, E], I32)
        XG = sb("XG", [P, 2, 2, ROW])
        XGT = sb("XGT", [P, 2, TILE])
        META_ROW = sb("META_ROW", [P, 4, 2], I32)
        META_W = sb("META_W", [P, 4, 2])
        WR = sb("WR", [P, 2, max(WCOLS)])
        HT = sb("HT", [P, 2, HID[1] // P, TILE])
        YS = sb("YS", [P, 2, 2, D])

        bank = [ctx.enter_context(nc.psum_tensor(f"bank{k}", [P, 512], F32)) for k in range(8)]
        ST, MB, PF, PG, PA, PO = bank[0:2], bank[2:4], bank[4], bank[5], bank[6], bank[7]

        (loaded, cx0, cx1, x_stats, x_rstd, x_norm, front_t, front_kept, qk_done, hi_done, hl_done, v_done,
         v_kept, sel_t, sel_kept, masked, m_banks, m_read, m_t, m_split, shift0, shift1, s_banks, exp_done,
         av_done, av_kept, o_t, o_kept, ok_t, ok_kept, wo_done, x_new, n_stats, n_rstd, n_norm, n_copied, n_t,
         n_kept, lg_done, lg_kept, dve_own, pool_own, act_own, set_dve, set_act, set_pool, shifted, exp_e,
         mask_ready, counted, ranked, tables_ready, copied, scattered, pads, xg0, xg1, w_loaded, w_kept, meta,
         xg_t, xg_kept, h_done, gelu_done, y_done, y_kept, sc0, sc1, sc2, sc3, y_loaded, combined, stored,
         settled) = (
            ctx.enter_context(nc.semaphore(n)) for n in """loaded cx0 cx1 x_stats x_rstd x_norm front_t
            front_kept qk_done hi_done hl_done v_done v_kept sel_t sel_kept masked m_banks m_read m_t m_split
            shift0 shift1 s_banks exp_done av_done av_kept o_t o_kept ok_t ok_kept wo_done x_new n_stats n_rstd
            n_norm n_copied n_t n_kept lg_done lg_kept dve_own pool_own act_own set_dve set_act set_pool
            shifted exp_e mask_ready counted ranked tables_ready copied scattered pads xg0 xg1 w_loaded w_kept
            meta xg_t xg_kept h_done gelu_done y_done y_kept sc0 sc1 sc2 sc3 y_loaded combined stored settled""".split())
        SHF, CXS, XGS = (shift0, shift1), (cx0, cx1), (xg0, xg1)
        SC = (sc0, sc1, sc2, sc3)

        def before(count):
            return max(count, 0) if isinstance(count, int) else count

        def settle(engine):
            engine.sem_inc(settled, 1)

        def const(name):
            a, b = at[name]
            return CONST[:, a:b]

        ident = const("ident")
        LOADS = 9
        SELF = WALL[:, E * WCOLS[0]:E * WCOLS[0] + 16 * 96]

        def pair_slots(engine, layer, slot, chain=None, links=0):
            def peeled(p):
                slot(lambda d: Pair(layer, (p + d) // 2, (p + d) % 2) if 0 <= p + d < PAIRS else None)

            for p in range(-4, 3):
                peeled(p)
            base = chain.before + chain.n if chain else 0
            with engine.Fori(0, (PAIRS - 8) // 2) as t:
                for k in (3, 4):
                    if chain:
                        chain.before, chain.n = base + (t * 2 + (k - 3)) * links, 0
                    slot(lambda d, k=k: Pair(layer, t + (k + d) // 2, (k + d) % 2))
                    assert not chain or chain.n == links, chain.n
            if chain:
                chain.before, chain.n = base + (PAIRS - 8) * links, 0
            for p in range(PAIRS - 5, PAIRS + 1):
                peeled(p)

        def tile_slots(engine, layer, slot, chain=None, links=0):
            n = TILES[layer]

            def peeled(i):
                slot(lambda d: Tile(layer, (i + d) // 4, (i + d) % 4) if 0 <= i + d < n else None)

            for i in range(-1, 5):
                peeled(i)
            base = chain.before + chain.n if chain else 0
            with engine.Fori(0, (n - 8) // 4) as t:
                for k in (5, 6, 7, 8):
                    if chain:
                        chain.before, chain.n = base + (t * 4 + (k - 5)) * links, 0
                    slot(lambda d, k=k: Tile(layer, t + (k + d) // 4, (k + d) % 4))
                    assert not chain or chain.n == links, chain.n
            if chain:
                chain.before, chain.n = base + (n - 8) * links, 0
            for i in range(n - 3, n + 1):
                peeled(i)

        block = ctx.enter_context(nc.Block())

        @block.sync
        def _(sp):
            loads = [(X[:, :].rearrange("p (b d) -> p b d", b=B), x_in.rearrange("b p d -> p b d")),
                     (CONST[:, :], const_in), (GATES[:, :], gates_in), (WSQ[:, :, :], wsq_in),
                     (WG[:, :, :], wg_in), (VEC[:, :], vec_in), (ROWS[:, :], rows_in),
                     (WALL[:, 0:E * WCOLS[0]], w0_in), (SELF, sel_in)]
            assert len(loads) == LOADS
            for to, of in loads:
                sp.dma_start(to, of).then_inc(loaded, 16)

            for layer in range(2):
                sp.dma_start(xs[layer][E * REG:, :], pads_in[E * TILE:, :]).then_inc(pads, 16)

            def attention_slot(pair):
                if a := pair(4):
                    sp.wait_ge(front_t, before(a.g - 1))
                    settle(sp)
                    sp.dma_start(CX[:, a.u, :].rearrange("p (c d) -> p c d", c=2),
                                 ctx_in[bass.ds(a.b, 2), :, :].rearrange("c p d -> p c d")).then_inc(CXS[a.u], 16)
                if a := pair(1):
                    sp.wait_ge(m_split, a.g + 1)
                    settle(sp)
                    sp.wait_ge(s_banks, before(8 * (a.g - 1)))
                    settle(sp)
                    for part in range(2):
                        sp.dma_start(QS[96 + part:97 + part, a.u, :, :, :].rearrange("o c h q -> o (c h) q"),
                                     MH[:, a.u, part, :]).then_inc(SHF[a.u], 16)

            def expert_layer(layer):
                sp.wait_ge(tables_ready, layer + 1)
                for e in range(E):
                    r = sp.value_load(CNTI[0:1, e:e + 1], min_val=0, max_val=T)
                    sp.dma_start(xs[layer][bass.ds(r + e * REG, TILE), :],
                                 pads_in[e * TILE:(e + 1) * TILE, :]).then_inc(pads, 16)
                sp.wait_ge(pads, 16 * (2 + E * (layer + 1)))
                sp.wait_ge(scattered, 16 * B * (1, 3)[layer])

                def slot(tile):
                    if a := tile(1):
                        sp.wait_ge(xg_t, before(a.g - 1))
                        settle(sp)
                        sp.wait_ge(meta, before(a.g - 1))
                        settle(sp)
                        r = sp.value_load(TBL[0:1, 0, bass.ds(a.i, 1)], min_val=0, max_val=E * REG + (E - 1) * TILE)
                        sp.dma_start(XG[:, a.u, :, :],
                                     xs[layer][bass.ds(r, TILE), :].rearrange("(p c) w -> p c w", c=2)).then_inc(XGS[a.u], 16)

                tile_slots(sp, layer, slot)
                for r in range(4):
                    sp.wait_ge(SC[r], 32 * (TILES[0] + TILES[1] * layer) // 4)
                if layer == 1:
                    sp.dma_start(N[:, :, 0:D], ys[1][T:2 * T, :].rearrange("(b p) d -> p b d", p=P)).then_inc(y_loaded, 16)
                sp.dma_start(N2[:, :, 0:D], ys[layer][0:T, :].rearrange("(b p) d -> p b d", p=P)).then_inc(y_loaded, 16)

            pair_slots(sp, 0, attention_slot)
            expert_layer(0)
            sp.dma_start(WALL[:, :], w1_in).then_inc(w_loaded, 16)
            pair_slots(sp, 1, attention_slot)
            expert_layer(1)
            sp.wait_ge(combined, 2)
            sp.dma_start(out.rearrange("b p d -> p b d"), X[:, :].rearrange("p (b d) -> p b d", b=B)).then_inc(stored, 16)
            sp.wait_ge(stored, 16)

        @block.gpsimd
        def _(pool):
            chain = Chain(pool, pool_own)
            nc.gpsimd.memset(KS[96:98, :, :, :], SHIFT).then_inc(set_pool, 1)
            pool.wait_ge(set_pool, 1)
            nc.gpsimd.memset(EXPO[:, :], -0.5).then_inc(set_pool, 1)
            pool.wait_ge(set_pool, 2)
            pool.wait_ge(loaded, 16 * LOADS)

            def rstd(ve, mv, to, done):
                settle(pool)
                chain.link(nc.gpsimd.tensor_scalar(out=ve, in0=mv, scalar1=LN_EPS, scalar2=None, op0=ALU.add))
                nc.gpsimd.tensor_tensor(out=to, in0=ve, in1=EXPO[:, :], op=ALU.pow).then_inc(done, 1)

            def attention_slot(pair):
                if a := pair(-1):
                    pool.wait_ge(n_norm, a.g + 1)
                    nc.gpsimd.tensor_copy(N[:, bass.ds(a.b, 2), 0:D],
                                          XN_N[:, a.u, :].rearrange("p (c d) -> p c d", c=2)).then_inc(n_copied, 1)
                if a := pair(0):
                    pool.wait_ge(n_stats, a.g + 1)
                    pool.wait_ge(n_norm, before(a.g - 1))
                    rstd(VE_N[:, :], MV_N[:, a.u, :, 1], RSTD_N[:, a.u, :], n_rstd)
                if a := pair(4):
                    pool.wait_ge(x_stats, a.g + 1)
                    pool.wait_ge(x_norm, before(a.g - 1))
                    rstd(VE[:, :], MV[:, a.u, :, 1], RSTD[:, a.u, :], x_rstd)

            def expert_layer(layer):
                pool.wait_ge(copied, layer + 1)
                pool.wait_ge(set_act, layer + 1)
                for k in range(layer + 1):
                    for b in range(B):
                        pool.indirect_dma_start(xs[layer][:, :], bass.IndirectOffsetOnAxis(ap=SLOT[:, k, b:b + 1], axis=0),
                                                (N, N2)[k][:, b, :], None).then_inc(scattered, 16)

                def slot(tile):
                    if a := tile(-1):
                        pool.wait_ge(y_kept, a.g + 1)
                        settle(pool)
                        for c in range(2):
                            pool.indirect_dma_start(ys[layer][:, :], bass.IndirectOffsetOnAxis(ap=META_ROW[:, a.r, c:c + 1], axis=0),
                                                    YS[:, a.u, c, :], None).then_inc(SC[a.r], 16)

                tile_slots(pool, layer, slot)

            for layer in range(2):
                pair_slots(pool, layer, attention_slot, chain, 2)
                expert_layer(layer)

        @block.scalar
        def _(act):
            chain = Chain(act, act_own)
            act.wait_ge(loaded, 16 * LOADS)
            nc.scalar.activation(GATES[:, :], GATES[:, :], ACT.Tanh).then_inc(act_own, 1)
            chain.n = 1

            def attention_slot(layer):
                def slot(pair):
                    if a := pair(0):
                        for c in range(2):
                            for g in range(G):
                                i = c * G + g
                                act.wait_ge(s_banks, 8 * a.g + i + 1)
                                if g == 0:
                                    act.wait_ge(av_done, before(2 * a.g + c - 1))
                                nc.scalar.activation(PT[:, c, 4 * g:4 * g + 4, :].rearrange("p j q -> p (j q)"),
                                                     ST[i % 2][:, :], ACT.Exp, scale=SCALE[layer]).then_inc(exp_done, 1)
                    if r := pair(2):
                        act.wait_ge(masked, r.g)
                        act.wait_ge(s_banks, before(8 * (r.g - 1)))
                        for k in range(4):
                            act.wait_ge(sel_t, 4 * r.g + k + 1)
                            to = (QL[:, 0:2], QL[:, 2:4], KS[0:96, r.u, 0:2], KS[0:96, r.u, 2:4])[k]
                            nc.scalar.activation(to.rearrange("p g n -> p (g n)"), (PG, PF)[k % 2][0:96, :],
                                                 ACT.Copy).then_inc(sel_kept, 1)
                    if b := pair(-1):
                        act.wait_ge(n_t, b.g + 1)
                        act.wait_ge(lg_done, b.g)
                        nc.scalar.activation(NT[:, :], PO[:, 0:256], ACT.Copy).then_inc(n_kept, 1)
                    if a:
                        keep_av(a, 0)
                    if f := pair(3):
                        act.wait_ge(front_t, f.g + 1)
                        act.wait_ge(v_done, before(f.g - 1))
                        nc.scalar.activation(XT[:, f.u, :], PF[:, :], ACT.Copy).then_inc(front_kept, 1)
                    if a:
                        keep_av(a, 1)
                    if b:
                        act.wait_ge(lg_done, b.g + 1)
                        nc.scalar.activation(LG[:, bass.ds(b.b * E, 2 * E)], PO[:, 384:384 + 2 * E], ACT.Copy).then_inc(lg_kept, 1)
                    if f:
                        act.wait_ge(qk_done, f.g + 1)
                        act.wait_ge(sel_t, before(4 * (f.g - 1)))
                        for k in range(2):
                            last = nc.scalar.activation(HL[:, f.u, 0, 256 * k:256 * k + 256], PG[:, 256 * k:256 * k + 256],
                                                        ACT.Identity, bias=VEC[:, 2 * D + 2 * layer + k:2 * D + 2 * layer + k + 1])
                        last.then_inc(hi_done, 1)
                    if a and layer == 0:
                        act.wait_ge(ok_t, a.g + 1)
                        act.wait_ge(wo_done, a.g)
                        nc.scalar.activation(OKT[:, :], PA[:, 0:256], ACT.Copy).then_inc(ok_kept, 1)
                return slot

            def keep_av(a, c):
                act.wait_ge(av_done, 2 * a.g + c + 1)
                act.wait_ge(o_t, before(2 * a.g + c - 1))
                nc.scalar.activation(OT[:, c, :], PA[:, :], ACT.Copy).then_inc(av_kept, 1)

            def expert_layer(layer):
                act.wait_ge(shifted, layer + 1)
                nc.scalar.activation(PR[:, :, :], PR[:, :, :], ACT.Exp).then_inc(exp_e, 1)
                if layer == 1:
                    act.wait_ge(n_copied, 2 * PAIRS)
                    nc.scalar.activation(N2[:, :, 0:D], N[:, :, 0:D], ACT.Copy).then_inc(set_act, 1)
                else:
                    nc.scalar.activation(NT[:, 0:1], NT[:, 0:1], ACT.Copy).then_inc(set_act, 1)

                def slot(tile):
                    if a := tile(1):
                        act.wait_ge(xg_t, a.g + 1)
                        act.wait_ge(h_done, before(a.hb - a.banks))
                        nc.scalar.activation(XGT[:, a.u, :], bank[4 + a.u][:, 0:TILE], ACT.Copy).then_inc(xg_kept, 1)
                    if a := tile(0):
                        act.wait_ge(y_done, before(a.g - 1))
                        if layer == 0:
                            act.wait_ge(h_done, a.hb + 1)
                            nc.scalar.activation(HT[:, a.u, 0:2, :].rearrange("p m n -> p (m n)"), bank[2 * a.u][:, :],
                                                 ACT.Gelu).then_inc(gelu_done, 1)
                        else:
                            for m in range(4):
                                if m % 2 == 0:
                                    act.wait_ge(h_done, a.hb + m // 2 + 1)
                                last = nc.scalar.activation(HT[:, a.u, m, :], bank[2 * a.u + m // 2][:, TILE * (m % 2):TILE * (m % 2) + TILE],
                                                            ACT.Gelu, bias=WR[:, a.u, 2 * HID[1] + m:2 * HID[1] + m + 1])
                            last.then_inc(gelu_done, 1)

                tile_slots(act, layer, slot)

            for layer in range(2):
                pair_slots(act, layer, attention_slot(layer))
                expert_layer(layer)

        @block.tensor
        def _(pe):
            pe.wait_ge(loaded, 16 * LOADS)
            pe.wait_ge(set_dve, 6)

            def transpose(to, of):
                return nc.tensor.transpose(to, of, ident)

            def attention_slot(layer):
                WQ, WK, WV = (WSQ[:, 4 * layer + k, :] for k in range(3))

                def slot(pair):
                    a, m, b, r, f = pair(0), pair(1), pair(-1), pair(2), pair(3)
                    if m:
                        pe.wait_ge(masked, m.g + 1)
                        pe.wait_ge(sel_kept, 4 * m.g + 4)
                    if a:
                        pe.wait_ge(SHF[a.u], 32 * (a.n + 1))
                    for c in range(2):
                        for g in range(G):
                            i = c * G + g
                            if a:
                                pe.wait_ge(exp_done, before(8 * a.g + i - 1))
                                nc.tensor.matmul(ST[i % 2][:, :].rearrange("p (j q) -> p j q", j=J),
                                                 KS[0:98, a.u, g, c * P:(c + 1) * P],
                                                 QS[0:98, a.u, c, J * g:J * g + J, :],
                                                 start=True, stop=True).then_inc(s_banks, 1)
                            if m:
                                pe.wait_ge(m_read, before(8 * m.g + i - 1))
                                for j in range(J):
                                    last = nc.tensor.matmul(MB[i % 2][:, j * P:(j + 1) * P],
                                                            QS[0:96, m.u, c, J * g + j, :],
                                                            KS[0:96, m.u, g, c * P:(c + 1) * P], start=True, stop=True)
                                last.then_inc(m_banks, 1)
                    if r:
                        pe.wait_ge(hl_done, r.g + 1)
                        pe.wait_ge(v_kept, r.g)
                        for k in range(4):
                            if k >= 2:
                                pe.wait_ge(sel_kept, before(4 * r.g + k - 1))
                            for g in (2 * (k % 2), 2 * (k % 2) + 1):
                                for part in range(2):
                                    last = nc.tensor.matmul((PG, PF)[k % 2][0:96, 256 * (g % 2):256 * (g % 2) + 256],
                                                            SEL[:, 2 * (k // 2) + part, g, :],
                                                            HL[:, r.u, part, 256 * (k // 2):256 * (k // 2) + 256],
                                                            start=(part == 0), stop=(part == 1))
                            last.then_inc(sel_t, 1)
                    if b:
                        pe.wait_ge(n_norm, b.g + 1)
                        pe.wait_ge(o_kept, 2 * b.g + 2)
                        for c in range(2):
                            last = transpose(PO[:, c * P:(c + 1) * P], XN_N[:, b.u, c * D:(c + 1) * D])
                        last.then_inc(n_t, 1)
                    if m:
                        pe.wait_ge(m_read, 8 * m.g + 8)
                        pe.wait_ge(m_split, m.g)
                        if r:
                            pe.wait_ge(sel_kept, 4 * r.g + 3)
                        transpose(PG[0:32, 0:P], MX[:, m.u, :]).then_inc(m_t, 1)
                    if a:
                        values(a, 0)
                    if f:
                        pe.wait_ge(x_norm, f.g + 1)
                        pe.wait_ge(CXS[f.u], 16 * (f.n + 1))
                        pe.wait_ge(sel_kept, 4 * f.g)
                        for c in range(4):
                            of = (XN if c < 2 else CX)[:, f.u, (c % 2) * D:(c % 2 + 1) * D]
                            last = transpose(PF[:, c * P:(c + 1) * P], of)
                        last.then_inc(front_t, 1)
                    if a:
                        values(a, 1)
                    if b:
                        pe.wait_ge(n_kept, b.g + 1)
                        for c in range(2):
                            last = nc.tensor.matmul(PO[:, 384 + E * c:384 + E * c + E], NT[:, c * P:(c + 1) * P],
                                                    WG[:, layer, :], start=True, stop=True)
                        last.then_inc(lg_done, 1)
                    if a:
                        if b:
                            pe.wait_ge(lg_kept, b.g + 1)
                        out_t(a, 0)
                    if f:
                        pe.wait_ge(front_kept, f.g + 1)
                        if m:
                            pe.wait_ge(m_split, m.g + 1)
                        nc.tensor.matmul(PG[:, 0:256], WQ, XT[:, f.u, 0:256], start=True, stop=True)
                        nc.tensor.matmul(PG[:, 256:512], WK, XT[:, f.u, 256:512], start=True,
                                         stop=True).then_inc(qk_done, 1)
                    if a:
                        out_t(a, 1)
                    if r:
                        pe.wait_ge(sel_kept, 4 * r.g + 4)
                        if f:
                            pe.wait_ge(front_kept, f.g + 1)
                        for c in range(2):
                            last = nc.tensor.matmul(PF[:, c * P:(c + 1) * P], XT[:, r.u, 256 + c * P:256 + (c + 1) * P],
                                                    WV, start=True, stop=True)
                        last.then_inc(v_done, 1)
                    if a:
                        if layer == 0:
                            pe.wait_ge(o_kept, 2 * a.g + 2)
                            pe.wait_ge(av_kept, 2 * a.g + 2)
                            for c in range(2):
                                last = transpose(PA[:, c * P:(c + 1) * P], OK[:, c * D:(c + 1) * D])
                            last.then_inc(ok_t, 1)
                            pe.wait_ge(ok_kept, a.g + 1)
                            for c in range(2):
                                last = nc.tensor.matmul(PA[:, 256 + c * P:256 + (c + 1) * P], OKT[:, c * P:(c + 1) * P],
                                                        WSQ[:, 3, :], start=True, stop=True)
                            last.then_inc(wo_done, 1)

                def values(a, c):
                    pe.wait_ge(exp_done, 8 * a.g + 4 * c + 4)
                    pe.wait_ge(v_kept, a.g + 1)
                    pe.wait_ge(av_kept, 2 * a.g + c)
                    if layer == 0 and c == 0:
                        pe.wait_ge(x_new, a.g)
                    for j in range(J):
                        for g in range(G):
                            last = nc.tensor.matmul(PA[32 * g:32 * g + 32, j * P:(j + 1) * P], VA[:, a.u, c, J * g + j, :],
                                                    PT[:, c, J * g + j, :], start=True, stop=True)
                    last.then_inc(av_done, 1)

                def out_t(a, c):
                    pe.wait_ge(av_kept, 2 * a.g + c + 1)
                    pe.wait_ge(o_kept, 2 * a.g + c)
                    for j in range(J):
                        last = transpose(PO[:, j * P:(j + 1) * P], OT[:, c, j * P:(j + 1) * P])
                    last.then_inc(o_t, 1)

                return slot

            def rank():
                nc.tensor.matmul(PF[:, 0:E * B], BEFORE[:, :], MASK[:, :, :].rearrange("p e b -> p (e b)"), start=True, stop=True)
                nc.tensor.matmul(PG[:, 0:E * B], ONES[:, :], MASK[:, :, :].rearrange("p e b -> p (e b)"), start=True,
                                 stop=True).then_inc(ranked, 1)

            def expert_layer(layer):
                if layer == 0:
                    with pe.Fori(0, TOP_BIT + 1) as t:
                        pe.wait_ge(mask_ready, t + 1)
                        nc.tensor.matmul(PO[:, 0:E], ONES[:, :], CN[:, :], start=True, stop=True).then_inc(counted, 1)
                    pe.wait_ge(mask_ready, TOP_BIT + 2)
                    nc.tensor.matmul(PO[:, 0:E], ONES[:, :], CN[:, :], start=True, stop=True)
                    rank()
                    pe.wait_ge(mask_ready, TOP_BIT + 3)
                    rank()
                else:
                    pe.wait_ge(mask_ready, TOP_BIT + 4)
                    rank()
                hid = HID[layer]
                M = hid // P

                def slot(tile):
                    if a := tile(1):
                        pe.wait_ge(XGS[a.u], 16 * (a.h + 1))
                        pe.wait_ge(xg_kept, before(a.g - 1))
                        for c in range(2):
                            last = transpose(bank[4 + a.u][:, c * P:(c + 1) * P], XG[:, a.u, c, 0:D])
                        last.then_inc(xg_t, 1)
                    if a := tile(0):
                        pe.wait_ge(xg_kept, a.g + 1)
                        pe.wait_ge(w_kept, a.g + 1)
                        pe.wait_ge(gelu_done, before(a.g - 1))
                        for m in range(M):
                            last = nc.tensor.matmul(bank[2 * a.u + m // 2][:, TILE * (m % 2):TILE * (m % 2) + TILE],
                                                    WR[:, a.u, m * P:(m + 1) * P], XGT[:, a.u, :], start=True, stop=True)
                            if m % 2:
                                last.then_inc(h_done, 1)
                    if a := tile(-1):
                        pe.wait_ge(gelu_done, a.g + 1)
                        pe.wait_ge(y_kept, before(a.g - 1))
                        for c in range(2):
                            for m in range(M):
                                last = nc.tensor.matmul(bank[6 + a.u][:, c * D:(c + 1) * D], HT[:, a.u, m, c * P:(c + 1) * P],
                                                        WR[:, a.u, hid + m * D:hid + (m + 1) * D], start=(m == 0), stop=(m == M - 1))
                        last.then_inc(y_done, 1)

                tile_slots(pe, layer, slot)

            for layer in range(2):
                pair_slots(pe, layer, attention_slot(layer))
                expert_layer(layer)

        @block.vector
        def _(dve):
            V = nc.vector
            chain = Chain(dve, dve_own)
            link = chain.link
            V.memset(VA[:, :, :, :, :], 0.0).then_inc(set_dve, 1)
            dve.wait_ge(set_dve, 1)
            V.memset(VA[:, :, :, :, HD:HD + 1], 1.0).then_inc(set_dve, 1)
            dve.wait_ge(loaded, 16 * LOADS)
            V.tensor_copy(BEFORE[:, :], const("before")).then_inc(set_dve, 1)
            V.tensor_copy(ONES[:, :], const("ones")).then_inc(set_dve, 1)
            dve.wait_ge(act_own, 1)
            V.tensor_scalar(out=VEC[:, D:2 * D], in0=VEC[:, D:2 * D], scalar1=GATES[:, 0:1], scalar2=None,
                            op0=ALU.mult).then_inc(set_dve, 1)
            V.tensor_copy(SEL[:, :, :, :].rearrange("p k g r -> p (k g r)"), SELF).then_inc(set_dve, 1)
            dve.wait_ge(set_dve, 6)

            def stats(x, tmp, mv, done):
                settle(dve)
                V.bn_stats(out=tmp[:, 0, :], in_=x(0))
                link(V.bn_stats(out=tmp[:, 1, :], in_=x(1)))
                settle(dve)
                for c in range(2):
                    last = V.bn_aggr(out=mv[:, c, :], in_=tmp[:, c, :])
                last.then_inc(done, 1)

            def normalize(x, mv, rstd, to, done):
                for c in range(2):
                    last = V.tensor_scalar(out=to[:, c * D:(c + 1) * D], in0=x(c), scalar1=mv[:, c, 0:1],
                                           scalar2=rstd[:, c:c + 1], op0=ALU.subtract, op1=ALU.mult)
                last.then_inc(done, 1)

            def row(a):
                return lambda c: X[:, bass.ds((a.b + c) * D, D)]

            def pair_cols(a):
                return X[:, bass.ds(a.b * D, 2 * D)]

            def attention_slot(layer):
                def slot(pair):
                    a, m, b, r, f = pair(0), pair(1), pair(-1), pair(2), pair(3)
                    if f:
                        dve.wait_ge(x_rstd, f.g + 1)
                        dve.wait_ge(front_t, before(f.g - 1))
                        normalize(row(f), MV[:, f.u], RSTD[:, f.u, :], XN[:, f.u, :], x_norm)
                    if b:
                        dve.wait_ge(n_rstd, b.g + 1)
                        dve.wait_ge(n_t, before(b.g - 1))
                        dve.wait_ge(n_copied, before(b.g - 1))
                        normalize(row(b), MV_N[:, b.u], RSTD_N[:, b.u, :], XN_N[:, b.u, :], n_norm)
                    if m:
                        dve.wait_ge(m_t, before(m.g - 1))
                        for i in range(2 * G):
                            dve.wait_ge(m_banks, 8 * m.g + i + 1)
                            V.tensor_reduce(out=MX[:, m.u, J * i:J * i + J], in_=MB[i % 2][:, :].rearrange("p (j k) -> p j k", j=J),
                                            op=ALU.max, axis=AX_X).then_inc(m_read, 1)
                        dve.wait_ge(m_t, m.g + 1)
                        dve.wait_ge(SHF[m.u], 32 * m.n)
                        link(V.tensor_scalar(out=MH[:, m.u, 0, :], in0=PG[0:32, 0:P], scalar1=-1.0 / SHIFT,
                                             scalar2=None, op0=ALU.mult))
                        V.scalar_tensor_tensor(out=MH[:, m.u, 1, :], in0=PG[0:32, 0:P], scalar=-1.0 / SHIFT,
                                               in1=MH[:, m.u, 0, :], op0=ALU.mult, op1=ALU.subtract).then_inc(m_split, 1)
                    if a:
                        normalized(a, 0, layer)
                    if f:
                        dve.wait_ge(hi_done, f.g + 1)
                        for k in range(2):
                            last = V.scalar_tensor_tensor(out=HL[:, f.u, 1, 256 * k:256 * k + 256], in0=PG[:, 256 * k:256 * k + 256],
                                                          scalar=VEC[:, 2 * D + 2 * layer + k:2 * D + 2 * layer + k + 1],
                                                          in1=HL[:, f.u, 0, 256 * k:256 * k + 256], op0=ALU.add, op1=ALU.subtract)
                        last.then_inc(hl_done, 1)
                    if a:
                        normalized(a, 1, layer)
                    if r:
                        dve.wait_ge(sel_kept, 4 * r.g + 2)
                        dve.wait_ge(s_banks, before(8 * (r.g - 1)))
                        for j in range(J):
                            last = V.tensor_scalar(out=QS[0:96, r.u, :, j:H:J, :], in0=QL[:, :, :].rearrange("r g (c q) -> r c g q", c=2),
                                                   scalar1=const("heads")[0:96, j:j + 1], scalar2=None, op0=ALU.mult)
                        last.then_inc(masked, 1)
                        dve.wait_ge(v_done, r.g + 1)
                        dve.wait_ge(av_done, before(2 * (r.g - 1)))
                        v_in = PF[:, 0:256].rearrange("p (c h d) -> p c h d", c=2, h=H)
                        v_out = VA[:, r.u, :, :, 0:HD]
                        if layer == 0:
                            bv = VEC[:, 0:D].rearrange("p (h d) -> p h d", h=H)
                            for c in range(2):
                                last = V.tensor_tensor(out=v_out[:, c], in0=v_in[:, c], in1=bv, op=ALU.add)
                        else:
                            last = V.tensor_copy(v_out, v_in)
                        last.then_inc(v_kept, 1)
                    if a:
                        if layer == 0:
                            dve.wait_ge(wo_done, a.g + 1)
                            link(V.scalar_tensor_tensor(out=pair_cols(a), in0=PA[:, 256:512], scalar=GATES[:, 0:1],
                                                        in1=pair_cols(a), op0=ALU.mult, op1=ALU.add))
                            V.tensor_tensor(out=pair_cols(a).rearrange("p (c d) -> p c d", c=2),
                                            in0=pair_cols(a).rearrange("p (c d) -> p c d", c=2),
                                            in1=VEC[:, D:2 * D].unsqueeze(1).broadcast_to([P, 2, D]), op=ALU.add).then_inc(x_new, 1)
                        else:
                            dve.wait_ge(o_kept, 2 * a.g + 2)
                            V.scalar_tensor_tensor(out=pair_cols(a), in0=OK[:, :], scalar=GATES[:, 1:2],
                                                   in1=pair_cols(a), op0=ALU.mult, op1=ALU.add).then_inc(x_new, 1)
                        dve.wait_ge(x_new, a.g + 1)
                        dve.wait_ge(n_rstd, before(a.g - 1))
                        stats(row(a), STATS_N, MV_N[:, a.u], n_stats)
                    if n := pair(4):
                        dve.wait_ge(x_rstd, before(n.g - 1))
                        stats(row(n), STATS, MV[:, n.u], x_stats)
                return slot

            def normalized(a, c, layer):
                dve.wait_ge(o_t, 2 * a.g + c + 1)
                if layer == 0 and c == 0:
                    dve.wait_ge(ok_t, a.g)
                o = PO[:, :].rearrange("p (j g w) -> p g j w", j=J, g=G)
                rc = RC[:, c, :].rearrange("p (g j) -> p g j", g=G)
                link(V.reciprocal(rc, o[:, :, :, HD]))
                V.tensor_tensor(out=OK[:, c * D:(c + 1) * D].rearrange("p (g j d) -> p g j d", g=G, j=J), in0=o[:, :, :, 0:HD],
                                in1=rc.unsqueeze(3).broadcast_to([P, G, J, HD]), op=ALU.mult).then_inc(o_kept, 1)

            def over_b(x):
                return x.unsqueeze(2).broadcast_to([P, E, B])

            def over_e(x):
                return x.unsqueeze(1).broadcast_to([P, E, B])

            def by_row(x):
                return x.rearrange("p e b -> p b e")

            def tt(out, a, b, op):
                link(V.tensor_tensor(out=out, in0=a, in1=b, op=op))

            def ts(out, a, s1, op0, s2=None, op1=None):
                link(V.tensor_scalar(out=out, in0=a, scalar1=s1, scalar2=s2, op0=op0, **({"op1": op1} if op1 else {})))

            def reduce(out, a, op):
                link(V.tensor_reduce(out=out, in_=a, op=op, axis=AX_X))

            pr = PR[:, :, :].rearrange("p b e -> p e b")
            ra, rb, rk, oh = RA[:, :, :], RB[:, :, :], RK[:, :, :], OH[:, :, :]
            sm = [SM[:, k, :] for k in range(8)]
            ex = [EX[:, k, :] for k in range(8)]
            less = over_b(const("expert_less_e"))

            def first_best(values, best, to):
                reduce(best, by_row(values), ALU.max)
                tt(rb, values, over_e(best), ALU.is_ge)
                tt(rb, rb, less, ALU.mult)
                reduce(sm[7], by_row(rb), ALU.min)
                tt(to, less, over_e(sm[7]), ALU.is_equal)

            def ranks(n):
                dve.wait_ge(ranked, n)
                link(V.tensor_tensor_scan(out=rk.rearrange("p e b -> p (e b)"), data0=const("segment"), data1=PG[:, 0:E * B],
                                          initial=0.0, op0=ALU.mult, op1=ALU.add))
                link(V.tensor_copy(ex[1], RK[:, :, B - 1]))
                tt(rk.rearrange("p e b -> p (e b)"), rk.rearrange("p e b -> p (e b)"), PG[:, 0:E * B], ALU.subtract)
                tt(rk.rearrange("p e b -> p (e b)"), rk.rearrange("p e b -> p (e b)"), PF[:, 0:E * B], ALU.add)

            def slot_of(choice, k):
                tt(rb, choice, rk, ALU.mult)
                reduce(sm[6], by_row(rb), ALU.add)
                link(V.tensor_copy(SLOT[:, k, :], sm[6]))

            def tables(layer):
                n = TILES[layer]
                link(V.tensor_copy(CNTI[:, :], ex[1]))
                steps = TT[:, 0, :, :].rearrange("p i e -> p (i e)")[:, 0:2 * E * E].rearrange("p (e k) -> p e k", e=E)
                tt(steps, ex[1].unsqueeze(2).broadcast_to([P, E, 2 * E]),
                   const("tile_steps").unsqueeze(1).broadcast_to([P, E, 2 * E]), ALU.is_gt)
                reduce(ex[2], steps, ALU.add)
                link(V.tensor_tensor_scan(out=ex[3], data0=const("segment8"), data1=ex[2], initial=0.0,
                                          op0=ALU.mult, op1=ALU.add))
                tt(ex[4], ex[3], ex[2], ALU.subtract)
                ts(ex[5], ex[4], -float(TILE), ALU.mult)
                tt(ex[5], ex[5], const("expert_region"), ALU.add)
                index = const("tile_index")[:, 0:n]
                t0, t1 = TT[:, 0, 0:n, :], TT[:, 1, 0:n, :]
                idx = index.unsqueeze(2).broadcast_to([P, n, E])

                def over_i(x):
                    return x.unsqueeze(1).broadcast_to([P, n, E])

                tv = [TV[:, k, 0:n] for k in range(4)]
                tt(t0, idx, over_i(ex[4]), ALU.is_ge)
                tt(t1, over_i(ex[3]), idx, ALU.is_gt)
                tt(t0, t0, t1, ALU.mult)
                reduce(tv[1], t0, ALU.add)
                tt(t1, t0, over_i(ex[5]), ALU.mult)
                reduce(tv[0], t1, ALU.add)
                spare = ex[3][:, E - 1:E]
                ts(spare, spare, -float(TILE), ALU.mult, float(E * REG), ALU.add)
                ts(tv[2], tv[1], -1.0, ALU.mult, 1.0, ALU.add)
                ts(tv[2], tv[2], spare, ALU.mult)
                tt(tv[0], tv[0], tv[2], ALU.add)
                ts(tv[2], index, float(TILE), ALU.mult)
                tt(tv[0], tv[0], tv[2], ALU.add)
                link(V.tensor_copy(TBL[:, 0, 0:n], tv[0]))
                tt(t1, t0, over_i(const("expert_less_e")), ALU.mult)
                reduce(tv[0], t1, ALU.add)
                ts(tv[1], tv[1], float(E), ALU.mult)
                tt(tv[0], tv[0], tv[1], ALU.add)
                ts(tv[0], tv[0], float(WCOLS[layer]), ALU.mult)
                V.tensor_copy(TBL[:, 1, 0:n], tv[0]).then_inc(tables_ready, 1)
                dve.wait_ge(tables_ready, layer + 1)

            def probabilities(layer):
                dve.wait_ge(lg_kept, PAIRS * (layer + 1))
                lg = LG[:, :].rearrange("p (b e) -> p b e", b=B)
                reduce(sm[0], lg, ALU.max)
                V.tensor_tensor(out=PR[:, :, :], in0=lg, in1=sm[0].unsqueeze(2).broadcast_to([P, B, E]),
                                op=ALU.subtract).then_inc(shifted, 1)
                dve.wait_ge(exp_e, layer + 1)
                reduce(sm[0], PR[:, :, :], ALU.add)
                link(V.reciprocal(sm[1], sm[0]))
                tt(PR[:, :, :], PR[:, :, :], sm[1].unsqueeze(2).broadcast_to([P, B, E]), ALU.mult)

            def fill(buffer, k, weight):
                link(V.tensor_copy(buffer[:, :, D].bitcast(I32), ROWS[:, k * B:(k + 1) * B]))
                link(V.tensor_copy(buffer[:, :, D + 1], weight))

            def route_by_experts():
                thr, cand, bit, step = (IV[:, k, :] for k in range(4))
                link(V.memset(thr, 0))
                link(V.memset(cand, 1 << TOP_BIT))
                link(V.memset(bit, 1 << (TOP_BIT - 1)))
                link(V.memset(BITF[:, :], float(1 << TOP_BIT)))
                base = chain.before + chain.n
                LINKS = 6
                with dve.Fori(0, TOP_BIT + 1) as t:
                    chain.before, chain.n = base + t * LINKS, 0
                    tt(ra, pr, over_b(cand.bitcast(F32)), ALU.is_ge)
                    V.tensor_reduce(out=CN[:, :], in_=ra, op=ALU.add, axis=AX_X).then_inc(mask_ready, 1)
                    dve.wait_ge(counted, t + 1)
                    ts(step, PO[:, 0:E], float(CAP), ALU.is_ge, BITF[:, :], ALU.mult)
                    tt(thr, thr, step, ALU.bitwise_or)
                    tt(cand, thr, bit, ALU.bitwise_or)
                    ts(bit, bit, 1, ALU.logical_shift_right)
                    ts(BITF[:, :], BITF[:, :], 0.5, ALU.mult)
                    assert chain.n == LINKS
                chain.before, chain.n = base + (TOP_BIT + 1) * LINKS, 0
                thr = thr.bitcast(F32)
                tt(ra, pr, over_b(thr), ALU.is_gt)
                tt(oh, pr, over_b(thr), ALU.is_equal)
                link(V.tensor_copy(MASK[:, :, :], oh))
                V.tensor_reduce(out=CN[:, :], in_=ra, op=ALU.add, axis=AX_X).then_inc(mask_ready, 1)
                ranks(1)
                ts(ex[0], PO[:, 0:E], -1.0, ALU.mult, float(CAP), ALU.add)
                tt(rk, rk, over_b(ex[0]), ALU.is_lt)
                tt(oh, oh, rk, ALU.mult)
                tt(ra, ra, oh, ALU.add)
                reduce(sm[2], by_row(ra), ALU.max)
                ts(sm[2], sm[2], -1.0, ALU.mult, 1.0, ALU.add)
                tt(rb, ra, over_e(sm[2]), ALU.max)
                tt(rk, pr, rb, ALU.mult)
                ts(rb, rb, -1.0, ALU.add)
                tt(rk, rk, rb, ALU.add)
                first_best(rk, sm[3], oh)
                V.tensor_copy(MASK[:, :, :], oh).then_inc(mask_ready, 1)
                ranks(2)
                tt(rk, rk, over_b(const("expert_region")), ALU.add)
                slot_of(oh, 0)
                fill(N, 0, sm[3])

            def route_by_tokens():
                first_best(pr, sm[3], oh)
                ts(rk, oh, -2.0, ALU.mult)
                tt(rk, rk, pr, ALU.add)
                first_best(rk, sm[4], ra)
                V.tensor_tensor(out=MASK[:, :, :], in0=oh, in1=ra, op=ALU.add).then_inc(mask_ready, 1)
                tt(sm[5], sm[3], sm[4], ALU.add)
                ts(sm[5], sm[5], 1e-9, ALU.add)
                link(V.reciprocal(sm[5], sm[5]))
                tt(sm[3], sm[3], sm[5], ALU.mult)
                tt(sm[4], sm[4], sm[5], ALU.mult)
                ranks(3)
                tt(rk, rk, over_b(const("expert_region")), ALU.add)
                slot_of(oh, 0)
                slot_of(ra, 1)
                fill(N, 0, sm[3])
                fill(N2, 1, sm[4])

            def expert_layer(layer):
                probabilities(layer)
                dve.wait_ge(n_copied, PAIRS * (layer + 1))
                (route_by_experts, route_by_tokens)[layer]()
                link(V.tensor_copy(ex[6], ex[1]))
                V.tensor_copy(ex[7], ex[6]).then_inc(copied, 1)
                tables(layer)
                W, hid = WCOLS[layer], HID[layer]
                if layer == 1:
                    dve.wait_ge(w_loaded, 16)

                def slot(tile):
                    if a := tile(-1):
                        dve.wait_ge(y_done, a.g + 1)
                        dve.wait_ge(meta, a.g + 1)
                        dve.wait_ge(w_kept, a.g + 1)
                        old = (a.r + 2) % 4
                        dve.wait_ge(SC[old], 32 * a.n if a.r < 2 else 32 * (a.n + 1))
                        y = bank[6 + a.u][:, 0:2 * D].rearrange("p (c d) -> p c d", c=2)
                        if layer == 1:
                            link(V.tensor_tensor(out=YS[:, a.u, :, :], in0=y,
                                                 in1=WR[:, a.u, W - D:W].unsqueeze(1).broadcast_to([P, 2, D]), op=ALU.add))
                            y = YS[:, a.u, :, :]
                        for c in range(2):
                            last = V.tensor_scalar(out=YS[:, a.u, c, :], in0=y[:, c], scalar1=META_W[:, a.r, c:c + 1],
                                                   scalar2=None, op0=ALU.mult)
                        last.then_inc(y_kept, 1)
                    if a := tile(1):
                        dve.wait_ge(y_done, before(a.g - 1))
                        dve.wait_ge(y_kept, before(a.g - 1))
                        r = dve.value_load(TBL[0:1, 1, bass.ds(a.i, 1)], min_val=0, max_val=(E - 1) * W)
                        V.tensor_copy(WR[:, a.u, 0:W], WALL[:, bass.ds(r, W)]).then_inc(w_kept, 1)
                        dve.wait_ge(XGS[a.u], 16 * (a.h + 1))
                        dve.wait_ge(SC[a.r], 32 * a.n)
                        V.tensor_copy(META_ROW[:, a.r, :], XG[:, a.u, :, D].bitcast(I32))
                        V.tensor_copy(META_W[:, a.r, :], XG[:, a.u, :, D + 1]).then_inc(meta, 1)

                tile_slots(dve, layer, slot, chain, layer)
                dve.wait_ge(y_loaded, 16 * (1, 3)[layer])
                CH = B // 4
                for k in range(4):
                    rows = slice(k * CH, (k + 1) * CH)
                    x = X[:, k * CH * D:(k + 1) * CH * D].rearrange("p (b d) -> p b d", b=CH)
                    if layer == 1:
                        link(V.tensor_tensor(out=N2[:, rows, 0:D], in0=N2[:, rows, 0:D], in1=N[:, rows, 0:D], op=ALU.add))
                    link(V.scalar_tensor_tensor(out=x, in0=N2[:, rows, 0:D], scalar=GATES[:, 2 + layer:3 + layer], in1=x,
                                                op0=ALU.mult, op1=ALU.add))
                V.tensor_copy(ex[7], ex[6]).then_inc(combined, 1)

            for layer in range(2):
                pair_slots(dve, layer, attention_slot(layer), chain, (6, 5)[layer])
                expert_layer(layer)


def kernel(x, ctx_1024, g_xattn, g_ffn, L0_xattn_Wq, L0_xattn_bq, L0_xattn_Wk, L0_xattn_bk, L0_xattn_Wv, L0_xattn_bv,
           L0_xattn_Wo, L0_xattn_bo, L0_ffn_Wg, L0_ffn_W1, L0_ffn_W2, L1_xattn_Wq, L1_xattn_Wkv, L1_ffn_gate_w, L1_ffn_w1,
           L1_ffn_b1, L1_ffn_w2, L1_ffn_b2):
    import concourse.bacc as bacc
    from concourse.bass_utils import run_bass_kernel_spmd

    f = lambda a: np.ascontiguousarray(a)
    over = lambda v: np.broadcast_to(np.asarray(v)[None, :], (P, v.shape[0]))
    at, const, sel, rows, pads = constants()
    Wkv = np.asarray(L1_xattn_Wkv)
    squares = [np.asarray(w).T for w in (L0_xattn_Wq, L0_xattn_Wk, L0_xattn_Wv, L0_xattn_Wo)]
    squares += [np.asarray(L1_xattn_Wq), Wkv[:, 0:D], Wkv[:, D:2 * D]]

    def experts(w1, w2):
        e, _, hid = w1.shape
        return [np.transpose(np.asarray(w1), (1, 0, 2)),
                np.transpose(np.asarray(w2).reshape(e, hid // P, P, D), (2, 0, 1, 3)).reshape(P, e, hid // P * D)]

    zero = np.zeros((P, 2), np.float32)
    b1 = np.transpose(np.asarray(L1_ffn_b1).reshape(E, HID[1] // P, P), (2, 0, 1))
    b2 = np.broadcast_to(np.asarray(L1_ffn_b2)[None], (P, E, D))
    arrays = {
        "x": f(x), "ctx": f(ctx_1024),
        "gates": f(np.concatenate([over(g_xattn), over(g_ffn)], axis=1)),
        "wsq": f(np.stack(squares, axis=1)),
        "wg": f(np.stack([np.asarray(L0_ffn_Wg), np.asarray(L1_ffn_gate_w).T], axis=1)),
        "vec": f(np.concatenate([over(L0_xattn_bv), over(L0_xattn_bo), np.asarray(L0_xattn_bq)[:, None],
                                 np.asarray(L0_xattn_bk)[:, None], zero], axis=1)),
        "w0": f(np.concatenate(experts(L0_ffn_W1, L0_ffn_W2), axis=2).reshape(P, -1)),
        "w1": f(np.concatenate(experts(L1_ffn_w1, L1_ffn_w2) + [b1, b2], axis=2).reshape(P, -1)),
        "const": f(const), "sel": f(sel), "rows": f(rows), "pads": f(pads),
    }
    nc = bacc.Bacc("TRN2", target_bir_lowering=False, num_devices=1)
    args = [nc.dram_tensor(f"in_{n}", a.shape, mybir.dt.from_np(a.dtype), kind="ExternalInput").ap() for n, a in arrays.items()]
    out = nc.dram_tensor("out", (B, P, D), F32, kind="ExternalOutput").ap()
    program(nc, at, *args, out)
    result = run_bass_kernel_spmd(nc, [{f"in_{n}": a for n, a in arrays.items()}], core_ids=[0])
    return result.results[0]["out"]
```

```python
from contextlib import ExitStack

import numpy as np

import concourse.bass as bass
from concourse import mybir

F32 = mybir.dt.float32
F16 = mybir.dt.float16
BF16 = mybir.dt.bfloat16
I32 = mybir.dt.int32
ALU = mybir.AluOpType
ACT = mybir.ActivationFunctionType
AX_X = mybir.AxisListType.X

P = 128
B = 32
D = 128
H = 16
HD = D // H
G = 4
J = 4
E = 8
T = B * P
PAIRS = B // 2
CAP = T // E
HID = (256, 512)
TILE = 256
TILES = (T // TILE + E, 2 * T // TILE + E)
REG = T + TILE
ROW = D + 2
PAD_ROW = 2 * T
LN_EPS = 1e-5
SHIFT = 16384.0
SCALE = (HD ** -0.5, D ** -0.5)
WCOLS = (2 * HID[0], 2 * HID[1] + HID[1] // P + D)
TOP_BIT = 29


def constants():
    p = np.arange(P)[:, None]
    q = np.arange(P)[None, :]
    one = np.ones((P, 1))
    parts = [
        ("ident", p == q),
        ("before", p < q),
        ("ones", np.ones((P, P))),
        ("segment", one * (np.arange(E * B)[None, :] % B != 0)),
        ("expert_less_e", one * (np.arange(E)[None, :] - E)),
        ("expert_region", one * (np.arange(E)[None, :] * REG)),
        ("tile_steps", one * (np.arange(2 * E)[None, :] * TILE)),
        ("tile_index", one * np.arange(max(TILES))[None, :]),
        ("segment8", one * (np.arange(E)[None, :] >= 0)),
        ("heads", (p % 32) // HD == np.arange(J)[None, :]),
    ]
    at, cols = {}, []
    n = 0
    for name, a in parts:
        a = np.asarray(a, np.float32) * np.ones((P, 1), np.float32)
        at[name] = (n, n + a.shape[1])
        n += a.shape[1]
        cols.append(a)
    tokens = (np.arange(B)[None, :] * P + p).astype(np.int32)
    rows = np.concatenate([tokens, tokens + T], axis=1).astype(np.int32)
    pads = np.zeros((2 * E * TILE, ROW), np.float32)
    pads[:, D] = (PAD_ROW + np.arange(2 * E * TILE)).astype(np.int32).view(np.float32)
    sel = np.zeros((P, 2, 2, G, 3, 32), np.float32)
    for k, parts_of in enumerate(((0, 0, 1), (0, 1, 0))):
        for s, part in enumerate(parts_of):
            for g in range(G):
                sel[32 * g + np.arange(32), k, part, g, s, np.arange(32)] = 1
    return at, np.concatenate(cols, axis=1), sel.reshape(P, -1), rows, pads


class Chain:

    def __init__(self, engine, sem):
        self.engine, self.sem, self.before, self.n = engine, sem, 0, 0

    def link(self, instruction):
        instruction.then_inc(self.sem, 1)
        self.n += 1
        self.engine.wait_ge(self.sem, self.before + self.n)


class Pair:

    def __init__(self, layer, quarter, r):
        self.r, self.u = r, r % 2
        self.n = quarter + (PAIRS // 4) * layer
        self.p = quarter * 4 + r
        self.g = self.n * 4 + r
        self.h = self.n * 2 + r // 2
        self.b = self.p * 2


class Tile:

    def __init__(self, layer, quarter, r):
        self.layer, self.r, self.u = layer, r, r % 2
        self.n = quarter + (TILES[0] // 4) * layer
        self.i = quarter * 4 + r
        self.g = self.n * 4 + r
        self.h = self.n * 2 + r // 2
        self.banks = 1 + layer
        self.hb = self.i * self.banks + TILES[0] * layer


def program(nc, at, x_in, ctx_in, gates_in, wsq_in, wg_in, vec_in, w0_in, w1_in, const_in,
            sel_in, rows_in, pads_in, out):
    xs = [nc.dram_tensor(f"dispatched{k}", [E * REG + E * TILE, ROW], F32, kind="Internal").ap() for k in (0, 1)]
    ys = [nc.dram_tensor(f"returned{k}", [PAD_ROW + 2 * E * TILE, D], F32, kind="Internal").ap() for k in (0, 1)]

    with ExitStack() as ctx:
        ctx.enter_context(nc.allow_low_precision(reason="counts up to 32 are exact in bfloat16"))

        def sb(name, shape, dt=F32):
            return ctx.enter_context(nc.sbuf_tensor(name, shape, dt))

        X = sb("X", [P, T])
        N = sb("N", [P, B, ROW])
        QS_N2 = sb("QS_N2", [P, 4 * H * P + 2 * B * ROW], F16)
        N2 = QS_N2[:, 4 * H * P:].bitcast(F32).rearrange("p (b w) -> p b w", b=B)
        CONST = sb("CONST", [P, const_in.shape[1]])
        GATES = sb("GATES", [P, 4])
        WSQ = sb("WSQ", [P, 7, D])
        WG = sb("WG", [P, 2, E])
        VEC = sb("VEC", [P, 2 * D + 4])
        LG = sb("LG", [P, B * E])
        BEFORE = sb("BEFORE", [P, P], BF16)
        ONES = sb("ONES", [P, P], BF16)
        ROWS = sb("ROWS", [P, 2 * B], I32)
        WALL = sb("WALL", [P, E * max(WCOLS)])
        CX = sb("CX", [P, 2, 2 * D])
        STATS = sb("STATS", [P, 2, 6])
        MV = sb("MV", [P, 2, 2, 2])
        EXPO = sb("EXPO", [P, 2])
        VE = sb("VE", [P, 2])
        RSTD = sb("RSTD", [P, 2, 2])
        STATS_N = sb("STATS_N", [P, 2, 6])
        MV_N = sb("MV_N", [P, 2, 2, 2])
        VE_N = sb("VE_N", [P, 2])
        RSTD_N = sb("RSTD_N", [P, 2, 2])
        XN = sb("XN", [P, 2, 2 * D])
        XN_N = sb("XN_N", [P, 2, 2 * D])
        XT_HL_WR = sb("XT_HL_WR", [P, 2 * max(WCOLS)])
        XT = XT_HL_WR[:, 0:8 * D].rearrange("p (u n) -> p u n", u=2)
        HL = XT_HL_WR[:, 8 * D:16 * D].bitcast(F16).rearrange("p (u k n) -> p u k n", u=2, k=2)
        SEL = sb("SEL", [P, 4, G, 96], F16)
        QL = sb("QL", [96, G, 2 * P], F16)
        QS = QS_N2[:, 0:8 * H * P].rearrange("p (r c h q) -> p r c h q", r=4, c=2, h=H)
        KS = sb("KS", [P, 4, G, 2 * P], F16)
        VA = sb("VA", [P, 4, 2, H, 32])
        MX = sb("MX", [P, 2, 32])
        MH = sb("MH", [32, 2, 2, P], F16)
        PT = sb("PT", [P, 2, H, P])
        OT = sb("OT", [P, 2, 4 * P])
        RC = sb("RC", [P, 2, H])
        OK = sb("OK", [P, 2 * D])
        OKT = sb("OKT", [P, 2 * D])
        NT = sb("NT", [P, 2 * D])
        PR = sb("PR", [P, B, E])
        RA = sb("RA", [P, E, B])
        RB = sb("RB", [P, E, B])
        RK = sb("RK", [P, E, B])
        OH = sb("OH", [P, E, B])
        MASK = sb("MASK", [P, E, B], BF16)
        SM = sb("SM", [P, 8, B])
        CN = sb("CN", [P, E], BF16)
        EX = sb("EX", [P, 8, E])
        IV = sb("IV", [P, 4, E], I32)
        BITF = sb("BITF", [P, 1])
        SLOT = sb("SLOT", [P, 2, B], I32)
        NTM = max(TILES)
        TT = sb("TT", [P, 3, NTM, E])
        TV = sb("TV", [P, 4, NTM])
        TBL = sb("TBL", [P, 2, NTM], I32)
        CNTI = sb("CNTI", [P, E], I32)
        XG = sb("XG", [P, 2, 2, ROW])
        XGT = sb("XGT", [P, 2, TILE])
        META_ROW = sb("META_ROW", [P, 4, 2], I32)
        META_W = sb("META_W", [P, 4, 2])
        WR = XT_HL_WR[:, :].rearrange("p (u n) -> p u n", u=2)
        HT = sb("HT", [P, 2, HID[1] // P, TILE])
        YS = sb("YS", [P, 2, 2, D])

        bank = [ctx.enter_context(nc.psum_tensor(f"bank{k}", [P, 512], F32)) for k in range(8)]
        ST, MB, PF, PG, PA, PO = bank[0:2], bank[2:4], bank[4], bank[5], bank[6], bank[7]

        (loaded, cx0, cx1, x_stats, x_rstd, x_norm, front_t, front_kept, qk_done, hi_done, hl_done, v_done,
         v_kept, sel_t, sel_kept, masked, m_banks, m_read, m_t, m_split, shift0, shift1, s_banks, exp_done,
         av_done, av_kept, o_t, o_kept, ok_t, ok_kept, wo_done, x_new, n_stats, n_rstd, n_norm, n_copied, n_t,
         n_kept, lg_done, lg_kept, dve_own, pool_own, act_own, set_dve, set_act, set_pool, shifted, exp_e,
         mask_ready, counted, ranked, tables_ready, copied, scattered, pads, xg0, xg1, w_loaded, w_kept, meta,
         xg_t, xg_kept, h_done, gelu_done, y_done, y_kept, sc0, sc1, sc2, sc3, y_loaded, combined, stored,
         settled) = (
            ctx.enter_context(nc.semaphore(n)) for n in """loaded cx0 cx1 x_stats x_rstd x_norm front_t
            front_kept qk_done hi_done hl_done v_done v_kept sel_t sel_kept masked m_banks m_read m_t m_split
            shift0 shift1 s_banks exp_done av_done av_kept o_t o_kept ok_t ok_kept wo_done x_new n_stats n_rstd
            n_norm n_copied n_t n_kept lg_done lg_kept dve_own pool_own act_own set_dve set_act set_pool
            shifted exp_e mask_ready counted ranked tables_ready copied scattered pads xg0 xg1 w_loaded w_kept
            meta xg_t xg_kept h_done gelu_done y_done y_kept sc0 sc1 sc2 sc3 y_loaded combined stored settled""".split())
        SHF, CXS, XGS = (shift0, shift1), (cx0, cx1), (xg0, xg1)
        SC = (sc0, sc1, sc2, sc3)

        def before(count):
            return max(count, 0) if isinstance(count, int) else count

        def settle(engine):
            engine.sem_inc(settled, 1)

        def const(name):
            a, b = at[name]
            return CONST[:, a:b]

        ident = const("ident")
        LOADS = 9
        SELF = WALL[:, E * WCOLS[0]:E * WCOLS[0] + 16 * 96]

        def pair_slots(engine, layer, slot, chain=None, links=0):
            def peeled(p):
                slot(lambda d: Pair(layer, (p + d) // 4, (p + d) % 4) if 0 <= p + d < PAIRS else None)

            for p in range(-4, 4):
                peeled(p)
            base = chain.before + chain.n if chain else 0
            with engine.Fori(0, (PAIRS - 8) // 4) as t:
                for k in (4, 5, 6, 7):
                    if chain:
                        chain.before, chain.n = base + (t * 4 + (k - 4)) * links, 0
                    slot(lambda d, k=k: Pair(layer, t + (k + d) // 4, (k + d) % 4))
                    assert not chain or chain.n == links, chain.n
            if chain:
                chain.before, chain.n = base + (PAIRS - 8) * links, 0
            for p in range(PAIRS - 4, PAIRS + 2):
                peeled(p)

        def tile_slots(engine, layer, slot, chain=None, links=0):
            n = TILES[layer]

            def peeled(i):
                slot(lambda d: Tile(layer, (i + d) // 4, (i + d) % 4) if 0 <= i + d < n else None)

            for i in range(-1, 5):
                peeled(i)
            base = chain.before + chain.n if chain else 0
            with engine.Fori(0, (n - 8) // 4) as t:
                for k in (5, 6, 7, 8):
                    if chain:
                        chain.before, chain.n = base + (t * 4 + (k - 5)) * links, 0
                    slot(lambda d, k=k: Tile(layer, t + (k + d) // 4, (k + d) % 4))
                    assert not chain or chain.n == links, chain.n
            if chain:
                chain.before, chain.n = base + (n - 8) * links, 0
            for i in range(n - 3, n + 1):
                peeled(i)

        block = ctx.enter_context(nc.Block())

        @block.sync
        def _(sp):
            loads = [(X[:, :].rearrange("p (b d) -> p b d", b=B), x_in.rearrange("b p d -> p b d")),
                     (CONST[:, :], const_in), (GATES[:, :], gates_in), (WSQ[:, :, :], wsq_in),
                     (WG[:, :, :], wg_in), (VEC[:, :], vec_in), (ROWS[:, :], rows_in),
                     (WALL[:, 0:E * WCOLS[0]], w0_in), (SELF, sel_in)]
            assert len(loads) == LOADS
            for to, of in loads:
                sp.dma_start(to, of).then_inc(loaded, 16)

            for layer in range(2):
                sp.dma_start(xs[layer][E * REG:, :], pads_in[E * TILE:, :]).then_inc(pads, 16)

            def attention_slot(pair):
                if a := pair(4):
                    sp.wait_ge(front_t, before(a.g - 1))
                    settle(sp)
                    sp.dma_start(CX[:, a.u, :].rearrange("p (c d) -> p c d", c=2),
                                 ctx_in[bass.ds(a.b, 2), :, :].rearrange("c p d -> p c d")).then_inc(CXS[a.u], 16)
                if a := pair(1):
                    sp.wait_ge(m_split, a.g + 1)
                    settle(sp)
                    sp.wait_ge(s_banks, before(8 * (a.g - 3)))
                    settle(sp)
                    for part in range(2):
                        sp.dma_start(QS[96 + part:97 + part, a.r, :, :, :].rearrange("o c h q -> o (c h) q"),
                                     MH[:, a.u, part, :]).then_inc(SHF[a.u], 16)

            def expert_layer(layer):
                sp.wait_ge(tables_ready, layer + 1)
                for e in range(E):
                    r = sp.value_load(CNTI[0:1, e:e + 1], min_val=0, max_val=T)
                    sp.dma_start(xs[layer][bass.ds(r + e * REG, TILE), :],
                                 pads_in[e * TILE:(e + 1) * TILE, :]).then_inc(pads, 16)
                sp.wait_ge(pads, 16 * (2 + E * (layer + 1)))
                sp.wait_ge(scattered, 16 * B * (1, 3)[layer])

                def slot(tile):
                    if a := tile(1):
                        sp.wait_ge(xg_t, before(a.g - 1))
                        settle(sp)
                        sp.wait_ge(meta, before(a.g - 1))
                        settle(sp)
                        r = sp.value_load(TBL[0:1, 0, bass.ds(a.i, 1)], min_val=0, max_val=E * REG + (E - 1) * TILE)
                        sp.dma_start(XG[:, a.u, :, :],
                                     xs[layer][bass.ds(r, TILE), :].rearrange("(p c) w -> p c w", c=2)).then_inc(XGS[a.u], 16)

                tile_slots(sp, layer, slot)
                for r in range(4):
                    sp.wait_ge(SC[r], 32 * (TILES[0] + TILES[1] * layer) // 4)
                if layer == 1:
                    sp.dma_start(N[:, :, 0:D], ys[1][T:2 * T, :].rearrange("(b p) d -> p b d", p=P)).then_inc(y_loaded, 16)
                sp.dma_start(N2[:, :, 0:D], ys[layer][0:T, :].rearrange("(b p) d -> p b d", p=P)).then_inc(y_loaded, 16)

            pair_slots(sp, 0, attention_slot)
            expert_layer(0)
            sp.dma_start(WALL[:, :], w1_in).then_inc(w_loaded, 16)
            pair_slots(sp, 1, attention_slot)
            expert_layer(1)
            sp.wait_ge(combined, 2)
            sp.dma_start(out.rearrange("b p d -> p b d"), X[:, :].rearrange("p (b d) -> p b d", b=B)).then_inc(stored, 16)
            sp.wait_ge(stored, 16)

        @block.gpsimd
        def _(pool):
            chain = Chain(pool, pool_own)
            nc.gpsimd.memset(KS[96:98, :, :, :], SHIFT).then_inc(set_pool, 1)
            pool.wait_ge(set_pool, 1)
            nc.gpsimd.memset(EXPO[:, :], -0.5).then_inc(set_pool, 1)
            pool.wait_ge(set_pool, 2)
            pool.wait_ge(loaded, 16 * LOADS)

            def rstd(ve, mv, to, done):
                settle(pool)
                chain.link(nc.gpsimd.tensor_scalar(out=ve, in0=mv, scalar1=LN_EPS, scalar2=None, op0=ALU.add))
                nc.gpsimd.tensor_tensor(out=to, in0=ve, in1=EXPO[:, :], op=ALU.pow).then_inc(done, 1)

            def attention_slot(pair):
                if z := pair(-2):
                    pool.wait_ge(n_norm, z.g + 1)
                    nc.gpsimd.tensor_copy(N[:, bass.ds(z.b, 2), 0:D],
                                          XN_N[:, z.u, :].rearrange("p (c d) -> p c d", c=2)).then_inc(n_copied, 1)
                if n := pair(4):
                    pool.wait_ge(x_stats, n.g + 1)
                    pool.wait_ge(x_norm, before(n.g - 1))
                    rstd(VE[:, :], MV[:, n.u, :, 1], RSTD[:, n.u, :], x_rstd)
                if b := pair(-1):
                    pool.wait_ge(n_stats, b.g + 1)
                    pool.wait_ge(n_norm, before(b.g - 1))
                    rstd(VE_N[:, :], MV_N[:, b.u, :, 1], RSTD_N[:, b.u, :], n_rstd)

            def expert_layer(layer):
                pool.wait_ge(copied, layer + 1)
                pool.wait_ge(set_act, layer + 1)
                for k in range(layer + 1):
                    for b in range(B):
                        pool.indirect_dma_start(xs[layer][:, :], bass.IndirectOffsetOnAxis(ap=SLOT[:, k, b:b + 1], axis=0),
                                                (N, N2)[k][:, b, :], None).then_inc(scattered, 16)

                def slot(tile):
                    if a := tile(-1):
                        pool.wait_ge(y_kept, a.g + 1)
                        settle(pool)
                        for c in range(2):
                            pool.indirect_dma_start(ys[layer][:, :], bass.IndirectOffsetOnAxis(ap=META_ROW[:, a.r, c:c + 1], axis=0),
                                                    YS[:, a.u, c, :], None).then_inc(SC[a.r], 16)

                tile_slots(pool, layer, slot)

            for layer in range(2):
                pair_slots(pool, layer, attention_slot, chain, 2)
                expert_layer(layer)

        @block.scalar
        def _(act):
            chain = Chain(act, act_own)
            act.wait_ge(loaded, 16 * LOADS)
            nc.scalar.activation(GATES[:, :], GATES[:, :], ACT.Tanh).then_inc(act_own, 1)
            chain.n = 1

            def attention_slot(layer):
                def slot(pair):
                    a, b, z, r, f = pair(0), pair(-1), pair(-2), pair(2), pair(3)

                    def exponentials(i):
                        c, g = i // G, i % G
                        if a:
                            act.wait_ge(s_banks, 8 * a.g + i + 1)
                            if g == 0:
                                act.wait_ge(av_done, before(2 * a.g + c - 1))
                            nc.scalar.activation(PT[:, c, 4 * g:4 * g + 4, :].rearrange("p j q -> p (j q)"),
                                                 ST[i % 2][:, :], ACT.Exp, scale=SCALE[layer]).then_inc(exp_done, 1)

                    def keep_stack(k):
                        if r:
                            act.wait_ge(sel_t, 4 * r.g + k + 1)
                            if k == 0:
                                act.wait_ge(masked, r.g)
                            if k == 2:
                                act.wait_ge(s_banks, before(8 * (r.g - 3)))
                            to = (QL[:, 0:2], QL[:, 2:4], KS[0:96, r.r, 0:2], KS[0:96, r.r, 2:4])[k]
                            nc.scalar.activation(to.rearrange("p g n -> p (g n)"), (PG, PF)[k // 2][0:96, :],
                                                 ACT.Copy).then_inc(sel_kept, 1)

                    if b:
                        keep_av(b, 1)
                    keep_stack(0)
                    exponentials(0)
                    keep_stack(1)
                    exponentials(1)
                    if f:
                        act.wait_ge(front_t, f.g + 1)
                        act.wait_ge(v_done, before(f.g - 1))
                        nc.scalar.activation(XT[:, f.u, :], PF[:, :], ACT.Copy).then_inc(front_kept, 1)
                    exponentials(2)
                    if b and layer == 0:
                        act.wait_ge(ok_t, b.g + 1)
                        act.wait_ge(wo_done, b.g)
                        nc.scalar.activation(OKT[:, :], PA[:, 0:256], ACT.Copy).then_inc(ok_kept, 1)
                    exponentials(3)
                    keep_stack(2)
                    if z:
                        act.wait_ge(n_t, z.g + 1)
                        act.wait_ge(lg_done, z.g)
                        nc.scalar.activation(NT[:, :], PO[:, 0:256], ACT.Copy).then_inc(n_kept, 1)
                    exponentials(4)
                    if f:
                        act.wait_ge(qk_done, f.g + 1)
                        act.wait_ge(sel_t, before(4 * (f.g - 1)))
                        for k in range(2):
                            last = nc.scalar.activation(HL[:, f.u, 0, 256 * k:256 * k + 256], PG[:, 256 * k:256 * k + 256],
                                                        ACT.Identity, bias=VEC[:, 2 * D + 2 * layer + k:2 * D + 2 * layer + k + 1])
                        last.then_inc(hi_done, 1)
                    exponentials(5)
                    keep_stack(3)
                    exponentials(6)
                    if a:
                        keep_av(a, 0)
                    if z:
                        act.wait_ge(lg_done, z.g + 1)
                        nc.scalar.activation(LG[:, bass.ds(z.b * E, 2 * E)], PO[:, 384:384 + 2 * E], ACT.Copy).then_inc(lg_kept, 1)
                    exponentials(7)
                return slot

            def keep_av(a, c):
                act.wait_ge(av_done, 2 * a.g + c + 1)
                act.wait_ge(o_t, before(2 * a.g + c - 1))
                nc.scalar.activation(OT[:, c, :], PA[:, :], ACT.Copy).then_inc(av_kept, 1)

            def expert_layer(layer):
                act.wait_ge(shifted, layer + 1)
                nc.scalar.activation(PR[:, :, :], PR[:, :, :], ACT.Exp).then_inc(exp_e, 1)
                if layer == 1:
                    act.wait_ge(n_copied, 2 * PAIRS)
                    nc.scalar.activation(N2[:, :, 0:D], N[:, :, 0:D], ACT.Copy).then_inc(set_act, 1)
                else:
                    nc.scalar.activation(NT[:, 0:1], NT[:, 0:1], ACT.Copy).then_inc(set_act, 1)

                def slot(tile):
                    if a := tile(1):
                        act.wait_ge(xg_t, a.g + 1)
                        act.wait_ge(h_done, before(a.hb - a.banks))
                        nc.scalar.activation(XGT[:, a.u, :], bank[4 + a.u][:, 0:TILE], ACT.Copy).then_inc(xg_kept, 1)
                    if a := tile(0):
                        act.wait_ge(y_done, before(a.g - 1))
                        if layer == 0:
                            act.wait_ge(h_done, a.hb + 1)
                            nc.scalar.activation(HT[:, a.u, 0:2, :].rearrange("p m n -> p (m n)"), bank[2 * a.u][:, :],
                                                 ACT.Gelu).then_inc(gelu_done, 1)
                        else:
                            for m in range(4):
                                if m % 2 == 0:
                                    act.wait_ge(h_done, a.hb + m // 2 + 1)
                                last = nc.scalar.activation(HT[:, a.u, m, :], bank[2 * a.u + m // 2][:, TILE * (m % 2):TILE * (m % 2) + TILE],
                                                            ACT.Gelu, bias=WR[:, a.u, 2 * HID[1] + m:2 * HID[1] + m + 1])
                            last.then_inc(gelu_done, 1)

                tile_slots(act, layer, slot)

            for layer in range(2):
                pair_slots(act, layer, attention_slot(layer))
                expert_layer(layer)

        @block.tensor
        def _(pe):
            pe.wait_ge(loaded, 16 * LOADS)
            pe.wait_ge(set_dve, 6)

            def transpose(to, of):
                return nc.tensor.transpose(to, of, ident)

            def attention_slot(layer):
                WQ, WK, WV = (WSQ[:, 4 * layer + k, :] for k in range(3))

                def slot(pair):
                    a, m, b, z, r, f = pair(0), pair(1), pair(-1), pair(-2), pair(2), pair(3)

                    def scores(i):
                        c, g = i // G, i % G
                        if a:
                            if i == 0:
                                pe.wait_ge(SHF[a.u], 32 * (a.h + 1))
                            pe.wait_ge(exp_done, before(8 * a.g + i - 1))
                            nc.tensor.matmul(ST[i % 2][:, :].rearrange("p (j q) -> p j q", j=J),
                                             KS[0:98, a.r, g, c * P:(c + 1) * P],
                                             QS[0:98, a.r, c, J * g:J * g + J, :],
                                             start=True, stop=True).then_inc(s_banks, 1)

                    def scores_for_maxima(i):
                        c, g = i // G, i % G
                        if m:
                            if i == 0:
                                pe.wait_ge(masked, m.g + 1)
                                pe.wait_ge(sel_kept, 4 * m.g + 4)
                                pe.wait_ge(m_split, m.g)
                            pe.wait_ge(m_read, before(8 * m.g + i - 1))
                            for j in range(J):
                                last = nc.tensor.matmul(MB[i % 2][:, j * P:(j + 1) * P],
                                                        QS[0:96, m.r, c, J * g + j, :],
                                                        KS[0:96, m.r, g, c * P:(c + 1) * P], start=True, stop=True)
                            last.then_inc(m_banks, 1)

                    def stacks(k):
                        if r:
                            if k == 0:
                                pe.wait_ge(hl_done, r.g + 1)
                            elif k == 2:
                                pe.wait_ge(v_kept, r.g + 1)
                            else:
                                pe.wait_ge(sel_kept, 4 * r.g + k)
                            if k == 2 and f:
                                pe.wait_ge(front_kept, f.g + 1)
                            for g in (2 * (k % 2), 2 * (k % 2) + 1):
                                for part in range(2):
                                    last = nc.tensor.matmul((PG, PF)[k // 2][0:96, 256 * (g % 2):256 * (g % 2) + 256],
                                                            SEL[:, 2 * (k // 2) + part, g, :],
                                                            HL[:, r.u, part, 256 * (k // 2):256 * (k // 2) + 256],
                                                            start=(part == 0), stop=(part == 1))
                            last.then_inc(sel_t, 1)

                    if z:
                        pe.wait_ge(lg_kept, z.g)
                    if b:
                        out_t(b, 0)
                    scores_for_maxima(0)
                    if b:
                        values(b, 1)
                    scores_for_maxima(1)
                    stacks(0)
                    scores_for_maxima(2)
                    if r:
                        pe.wait_ge(front_kept, r.g + 1)
                        pe.wait_ge(sel_kept, 4 * r.g)
                        for c in range(2):
                            last = nc.tensor.matmul(PF[:, c * P:(c + 1) * P], XT[:, r.u, 256 + c * P:256 + (c + 1) * P],
                                                    WV, start=True, stop=True)
                        last.then_inc(v_done, 1)
                    scores(0)
                    scores_for_maxima(3)
                    if b:
                        out_t(b, 1)
                    stacks(1)
                    scores(1)
                    scores_for_maxima(4)
                    if f:
                        pe.wait_ge(x_norm, f.g + 1)
                        pe.wait_ge(CXS[f.u], 16 * (f.h + 1))
                        if r:
                            pe.wait_ge(v_kept, r.g + 1)
                        for c in range(4):
                            of = (XN if c < 2 else CX)[:, f.u, (c % 2) * D:(c % 2 + 1) * D]
                            last = transpose(PF[:, c * P:(c + 1) * P], of)
                        last.then_inc(front_t, 1)
                    scores(2)
                    scores_for_maxima(5)
                    if b and layer == 0:
                        pe.wait_ge(o_kept, 2 * b.g + 2)
                        pe.wait_ge(av_kept, 2 * b.g + 2)
                        for c in range(2):
                            last = transpose(PA[:, c * P:(c + 1) * P], OK[:, c * D:(c + 1) * D])
                        last.then_inc(ok_t, 1)
                    scores(3)
                    scores_for_maxima(6)
                    stacks(2)
                    if z:
                        pe.wait_ge(n_norm, z.g + 1)
                        if b:
                            pe.wait_ge(o_kept, 2 * b.g + 2)
                        for c in range(2):
                            last = transpose(PO[:, c * P:(c + 1) * P], XN_N[:, z.u, c * D:(c + 1) * D])
                        last.then_inc(n_t, 1)
                    scores(4)
                    scores_for_maxima(7)
                    if b and layer == 0:
                        pe.wait_ge(ok_kept, b.g + 1)
                        for c in range(2):
                            last = nc.tensor.matmul(PA[:, 256 + c * P:256 + (c + 1) * P], OKT[:, c * P:(c + 1) * P],
                                                    WSQ[:, 3, :], start=True, stop=True)
                        last.then_inc(wo_done, 1)
                    if f:
                        pe.wait_ge(front_kept, f.g + 1)
                        if r:
                            pe.wait_ge(sel_kept, 4 * r.g + 2)
                        nc.tensor.matmul(PG[:, 0:256], WQ, XT[:, f.u, 0:256], start=True, stop=True)
                        nc.tensor.matmul(PG[:, 256:512], WK, XT[:, f.u, 256:512], start=True,
                                         stop=True).then_inc(qk_done, 1)
                    scores(5)
                    stacks(3)
                    if m:
                        pe.wait_ge(m_read, 8 * m.g + 8)
                        transpose(MB[0][0:32, 0:P], MX[:, m.u, :]).then_inc(m_t, 1)
                    scores(6)
                    if a:
                        values(a, 0)
                    if z:
                        pe.wait_ge(n_kept, z.g + 1)
                        for c in range(2):
                            last = nc.tensor.matmul(PO[:, 384 + E * c:384 + E * c + E], NT[:, c * P:(c + 1) * P],
                                                    WG[:, layer, :], start=True, stop=True)
                        last.then_inc(lg_done, 1)
                    scores(7)

                def values(a, c):
                    pe.wait_ge(exp_done, 8 * a.g + 4 * c + 4)
                    pe.wait_ge(v_kept, a.g + 1)
                    pe.wait_ge(av_kept, 2 * a.g + c)
                    if layer == 0 and c == 0:
                        pe.wait_ge(x_new, a.g)
                    for j in range(J):
                        for g in range(G):
                            last = nc.tensor.matmul(PA[32 * g:32 * g + 32, j * P:(j + 1) * P], VA[:, a.r, c, J * g + j, :],
                                                    PT[:, c, J * g + j, :], start=True, stop=True)
                    last.then_inc(av_done, 1)

                def out_t(a, c):
                    pe.wait_ge(av_kept, 2 * a.g + c + 1)
                    pe.wait_ge(o_kept, 2 * a.g + c)
                    for j in range(J):
                        last = transpose(PO[:, j * P:(j + 1) * P], OT[:, c, j * P:(j + 1) * P])
                    last.then_inc(o_t, 1)

                return slot

            def rank():
                nc.tensor.matmul(PF[:, 0:E * B], BEFORE[:, :], MASK[:, :, :].rearrange("p e b -> p (e b)"), start=True, stop=True)
                nc.tensor.matmul(PG[:, 0:E * B], ONES[:, :], MASK[:, :, :].rearrange("p e b -> p (e b)"), start=True,
                                 stop=True).then_inc(ranked, 1)

            def expert_layer(layer):
                if layer == 0:
                    with pe.Fori(0, TOP_BIT + 1) as t:
                        pe.wait_ge(mask_ready, t + 1)
                        nc.tensor.matmul(PO[:, 0:E], ONES[:, :], CN[:, :], start=True, stop=True).then_inc(counted, 1)
                    pe.wait_ge(mask_ready, TOP_BIT + 2)
                    nc.tensor.matmul(PO[:, 0:E], ONES[:, :], CN[:, :], start=True, stop=True)
                    rank()
                    pe.wait_ge(mask_ready, TOP_BIT + 3)
                    rank()
                else:
                    pe.wait_ge(mask_ready, TOP_BIT + 4)
                    rank()
                hid = HID[layer]
                M = hid // P

                def slot(tile):
                    if a := tile(1):
                        pe.wait_ge(XGS[a.u], 16 * (a.h + 1))
                        pe.wait_ge(xg_kept, before(a.g - 1))
                        for c in range(2):
                            last = transpose(bank[4 + a.u][:, c * P:(c + 1) * P], XG[:, a.u, c, 0:D])
                        last.then_inc(xg_t, 1)
                    if a := tile(0):
                        pe.wait_ge(xg_kept, a.g + 1)
                        pe.wait_ge(w_kept, a.g + 1)
                        pe.wait_ge(gelu_done, before(a.g - 1))
                        for m in range(M):
                            last = nc.tensor.matmul(bank[2 * a.u + m // 2][:, TILE * (m % 2):TILE * (m % 2) + TILE],
                                                    WR[:, a.u, m * P:(m + 1) * P], XGT[:, a.u, :], start=True, stop=True)
                            if m % 2:
                                last.then_inc(h_done, 1)
                    if a := tile(-1):
                        pe.wait_ge(gelu_done, a.g + 1)
                        pe.wait_ge(y_kept, before(a.g - 1))
                        for c in range(2):
                            for m in range(M):
                                last = nc.tensor.matmul(bank[6 + a.u][:, c * D:(c + 1) * D], HT[:, a.u, m, c * P:(c + 1) * P],
                                                        WR[:, a.u, hid + m * D:hid + (m + 1) * D], start=(m == 0), stop=(m == M - 1))
                        last.then_inc(y_done, 1)

                tile_slots(pe, layer, slot)

            for layer in range(2):
                pair_slots(pe, layer, attention_slot(layer))
                expert_layer(layer)

        @block.vector
        def _(dve):
            V = nc.vector
            chain = Chain(dve, dve_own)
            link = chain.link
            V.memset(VA[:, :, :, :, :], 0.0).then_inc(set_dve, 1)
            dve.wait_ge(set_dve, 1)
            V.memset(VA[:, :, :, :, HD:HD + 1], 1.0).then_inc(set_dve, 1)
            dve.wait_ge(loaded, 16 * LOADS)
            V.tensor_copy(BEFORE[:, :], const("before")).then_inc(set_dve, 1)
            V.tensor_copy(ONES[:, :], const("ones")).then_inc(set_dve, 1)
            dve.wait_ge(act_own, 1)
            V.tensor_scalar(out=VEC[:, D:2 * D], in0=VEC[:, D:2 * D], scalar1=GATES[:, 0:1], scalar2=None,
                            op0=ALU.mult).then_inc(set_dve, 1)
            V.tensor_copy(SEL[:, :, :, :].rearrange("p k g r -> p (k g r)"), SELF).then_inc(set_dve, 1)
            dve.wait_ge(set_dve, 6)

            def stats(x, tmp, mv, done):
                settle(dve)
                V.bn_stats(out=tmp[:, 0, :], in_=x(0))
                link(V.bn_stats(out=tmp[:, 1, :], in_=x(1)))
                settle(dve)
                for c in range(2):
                    last = V.bn_aggr(out=mv[:, c, :], in_=tmp[:, c, :])
                last.then_inc(done, 1)

            def normalize(x, mv, rstd, to, done):
                for c in range(2):
                    last = V.tensor_scalar(out=to[:, c * D:(c + 1) * D], in0=x(c), scalar1=mv[:, c, 0:1],
                                           scalar2=rstd[:, c:c + 1], op0=ALU.subtract, op1=ALU.mult)
                last.then_inc(done, 1)

            def row(a):
                return lambda c: X[:, bass.ds((a.b + c) * D, D)]

            def pair_cols(a):
                return X[:, bass.ds(a.b * D, 2 * D)]

            def attention_slot(layer):
                def slot(pair):
                    m, b, z, r, f, n = pair(1), pair(-1), pair(-2), pair(2), pair(3), pair(4)

                    def maxima(i):
                        if m:
                            if i == 0:
                                dve.wait_ge(m_t, before(m.g - 1))
                            dve.wait_ge(m_banks, 8 * m.g + i + 1)
                            V.tensor_reduce(out=MX[:, m.u, J * i:J * i + J], in_=MB[i % 2][:, :].rearrange("p (j k) -> p j k", j=J),
                                            op=ALU.max, axis=AX_X).then_inc(m_read, 1)

                    def blocks(js):
                        if r:
                            for j in js:
                                last = V.tensor_scalar(out=QS[0:96, r.r, :, j:H:J, :], in0=QL[:, :, :].rearrange("r g (c q) -> r c g q", c=2),
                                                       scalar1=const("heads")[0:96, j:j + 1], scalar2=None, op0=ALU.mult)
                            if J - 1 in js:
                                last.then_inc(masked, 1)

                    maxima(0)
                    if b:
                        normalized(b, 0, layer)
                    maxima(1)
                    if f:
                        dve.wait_ge(x_rstd, f.g + 1)
                        dve.wait_ge(front_t, before(f.g - 1))
                        normalize(row(f), MV[:, f.u], RSTD[:, f.u, :], XN[:, f.u, :], x_norm)
                    maxima(2)
                    if r:
                        dve.wait_ge(v_done, r.g + 1)
                        dve.wait_ge(av_done, before(2 * (r.g - 3)))
                        v_in = PF[:, 0:256].rearrange("p (c h d) -> p c h d", c=2, h=H)
                        v_out = VA[:, r.r, :, :, 0:HD]
                        if layer == 0:
                            bv = VEC[:, 0:D].rearrange("p (h d) -> p h d", h=H)
                            for c in range(2):
                                last = V.tensor_tensor(out=v_out[:, c], in0=v_in[:, c], in1=bv, op=ALU.add)
                        else:
                            last = V.tensor_copy(v_out, v_in)
                        last.then_inc(v_kept, 1)
                    maxima(3)
                    if z:
                        dve.wait_ge(n_rstd, z.g + 1)
                        dve.wait_ge(n_t, before(z.g - 1))
                        dve.wait_ge(n_copied, before(z.g - 1))
                        normalize(row(z), MV_N[:, z.u], RSTD_N[:, z.u, :], XN_N[:, z.u, :], n_norm)
                    if b:
                        normalized(b, 1, layer)
                    maxima(4)
                    if r:
                        dve.wait_ge(sel_kept, 4 * r.g + 2)
                        dve.wait_ge(s_banks, before(8 * (r.g - 3)))
                    blocks((0, 1))
                    maxima(5)
                    blocks((2, 3))
                    maxima(6)
                    if n:
                        dve.wait_ge(x_rstd, before(n.g - 1))
                        stats(row(n), STATS, MV[:, n.u], x_stats)
                    maxima(7)
                    if b:
                        if layer == 0:
                            dve.wait_ge(wo_done, b.g + 1)
                            link(V.scalar_tensor_tensor(out=pair_cols(b), in0=PA[:, 256:512], scalar=GATES[:, 0:1],
                                                        in1=pair_cols(b), op0=ALU.mult, op1=ALU.add))
                            V.tensor_tensor(out=pair_cols(b).rearrange("p (c d) -> p c d", c=2),
                                            in0=pair_cols(b).rearrange("p (c d) -> p c d", c=2),
                                            in1=VEC[:, D:2 * D].unsqueeze(1).broadcast_to([P, 2, D]), op=ALU.add).then_inc(x_new, 1)
                        else:
                            dve.wait_ge(o_kept, 2 * b.g + 2)
                            V.scalar_tensor_tensor(out=pair_cols(b), in0=OK[:, :], scalar=GATES[:, 1:2],
                                                   in1=pair_cols(b), op0=ALU.mult, op1=ALU.add).then_inc(x_new, 1)
                    if m:
                        dve.wait_ge(m_t, m.g + 1)
                        dve.wait_ge(SHF[m.u], 32 * m.h)
                        link(V.tensor_scalar(out=MH[:, m.u, 0, :], in0=MB[0][0:32, 0:P], scalar1=-1.0 / SHIFT,
                                             scalar2=None, op0=ALU.mult))
                        V.scalar_tensor_tensor(out=MH[:, m.u, 1, :], in0=MB[0][0:32, 0:P], scalar=-1.0 / SHIFT,
                                               in1=MH[:, m.u, 0, :], op0=ALU.mult, op1=ALU.subtract).then_inc(m_split, 1)
                    if f:
                        dve.wait_ge(hi_done, f.g + 1)
                        for k in range(2):
                            last = V.scalar_tensor_tensor(out=HL[:, f.u, 1, 256 * k:256 * k + 256], in0=PG[:, 256 * k:256 * k + 256],
                                                          scalar=VEC[:, 2 * D + 2 * layer + k:2 * D + 2 * layer + k + 1],
                                                          in1=HL[:, f.u, 0, 256 * k:256 * k + 256], op0=ALU.add, op1=ALU.subtract)
                        last.then_inc(hl_done, 1)
                    if b:
                        dve.wait_ge(x_new, b.g + 1)
                        dve.wait_ge(n_rstd, before(b.g - 1))
                        stats(row(b), STATS_N, MV_N[:, b.u], n_stats)
                return slot

            def normalized(a, c, layer):
                dve.wait_ge(o_t, 2 * a.g + c + 1)
                if layer == 0 and c == 0:
                    dve.wait_ge(ok_t, a.g)
                o = PO[:, :].rearrange("p (j g w) -> p g j w", j=J, g=G)
                rc = RC[:, c, :].rearrange("p (g j) -> p g j", g=G)
                link(V.reciprocal(rc, o[:, :, :, HD]))
                V.tensor_tensor(out=OK[:, c * D:(c + 1) * D].rearrange("p (g j d) -> p g j d", g=G, j=J), in0=o[:, :, :, 0:HD],
                                in1=rc.unsqueeze(3).broadcast_to([P, G, J, HD]), op=ALU.mult).then_inc(o_kept, 1)

            def over_b(x):
                return x.unsqueeze(2).broadcast_to([P, E, B])

            def over_e(x):
                return x.unsqueeze(1).broadcast_to([P, E, B])

            def by_row(x):
                return x.rearrange("p e b -> p b e")

            def tt(out, a, b, op):
                link(V.tensor_tensor(out=out, in0=a, in1=b, op=op))

            def ts(out, a, s1, op0, s2=None, op1=None):
                link(V.tensor_scalar(out=out, in0=a, scalar1=s1, scalar2=s2, op0=op0, **({"op1": op1} if op1 else {})))

            def reduce(out, a, op):
                link(V.tensor_reduce(out=out, in_=a, op=op, axis=AX_X))

            pr = PR[:, :, :].rearrange("p b e -> p e b")
            ra, rb, rk, oh = RA[:, :, :], RB[:, :, :], RK[:, :, :], OH[:, :, :]
            sm = [SM[:, k, :] for k in range(8)]
            ex = [EX[:, k, :] for k in range(8)]
            less = over_b(const("expert_less_e"))

            def first_best(values, best, to):
                reduce(best, by_row(values), ALU.max)
                tt(rb, values, over_e(best), ALU.is_ge)
                tt(rb, rb, less, ALU.mult)
                reduce(sm[7], by_row(rb), ALU.min)
                tt(to, less, over_e(sm[7]), ALU.is_equal)

            def ranks(n):
                dve.wait_ge(ranked, n)
                link(V.tensor_tensor_scan(out=rk.rearrange("p e b -> p (e b)"), data0=const("segment"), data1=PG[:, 0:E * B],
                                          initial=0.0, op0=ALU.mult, op1=ALU.add))
                link(V.tensor_copy(ex[1], RK[:, :, B - 1]))
                tt(rk.rearrange("p e b -> p (e b)"), rk.rearrange("p e b -> p (e b)"), PG[:, 0:E * B], ALU.subtract)
                tt(rk.rearrange("p e b -> p (e b)"), rk.rearrange("p e b -> p (e b)"), PF[:, 0:E * B], ALU.add)

            def slot_of(choice, k):
                tt(rb, choice, rk, ALU.mult)
                reduce(sm[6], by_row(rb), ALU.add)
                link(V.tensor_copy(SLOT[:, k, :], sm[6]))

            def tables(layer):
                n = TILES[layer]
                link(V.tensor_copy(CNTI[:, :], ex[1]))
                steps = TT[:, 0, :, :].rearrange("p i e -> p (i e)")[:, 0:2 * E * E].rearrange("p (e k) -> p e k", e=E)
                tt(steps, ex[1].unsqueeze(2).broadcast_to([P, E, 2 * E]),
                   const("tile_steps").unsqueeze(1).broadcast_to([P, E, 2 * E]), ALU.is_gt)
                reduce(ex[2], steps, ALU.add)
                link(V.tensor_tensor_scan(out=ex[3], data0=const("segment8"), data1=ex[2], initial=0.0,
                                          op0=ALU.mult, op1=ALU.add))
                tt(ex[4], ex[3], ex[2], ALU.subtract)
                ts(ex[5], ex[4], -float(TILE), ALU.mult)
                tt(ex[5], ex[5], const("expert_region"), ALU.add)
                index = const("tile_index")[:, 0:n]
                t0, t1 = TT[:, 0, 0:n, :], TT[:, 1, 0:n, :]
                idx = index.unsqueeze(2).broadcast_to([P, n, E])

                def over_i(x):
                    return x.unsqueeze(1).broadcast_to([P, n, E])

                tv = [TV[:, k, 0:n] for k in range(4)]
                tt(t0, idx, over_i(ex[4]), ALU.is_ge)
                tt(t1, over_i(ex[3]), idx, ALU.is_gt)
                tt(t0, t0, t1, ALU.mult)
                reduce(tv[1], t0, ALU.add)
                tt(t1, t0, over_i(ex[5]), ALU.mult)
                reduce(tv[0], t1, ALU.add)
                spare = ex[3][:, E - 1:E]
                ts(spare, spare, -float(TILE), ALU.mult, float(E * REG), ALU.add)
                ts(tv[2], tv[1], -1.0, ALU.mult, 1.0, ALU.add)
                ts(tv[2], tv[2], spare, ALU.mult)
                tt(tv[0], tv[0], tv[2], ALU.add)
                ts(tv[2], index, float(TILE), ALU.mult)
                tt(tv[0], tv[0], tv[2], ALU.add)
                link(V.tensor_copy(TBL[:, 0, 0:n], tv[0]))
                tt(t1, t0, over_i(const("expert_less_e")), ALU.mult)
                reduce(tv[0], t1, ALU.add)
                ts(tv[1], tv[1], float(E), ALU.mult)
                tt(tv[0], tv[0], tv[1], ALU.add)
                ts(tv[0], tv[0], float(WCOLS[layer]), ALU.mult)
                V.tensor_copy(TBL[:, 1, 0:n], tv[0]).then_inc(tables_ready, 1)
                dve.wait_ge(tables_ready, layer + 1)

            def probabilities(layer):
                dve.wait_ge(lg_kept, PAIRS * (layer + 1))
                lg = LG[:, :].rearrange("p (b e) -> p b e", b=B)
                reduce(sm[0], lg, ALU.max)
                V.tensor_tensor(out=PR[:, :, :], in0=lg, in1=sm[0].unsqueeze(2).broadcast_to([P, B, E]),
                                op=ALU.subtract).then_inc(shifted, 1)
                dve.wait_ge(exp_e, layer + 1)
                reduce(sm[0], PR[:, :, :], ALU.add)
                link(V.reciprocal(sm[1], sm[0]))
                tt(PR[:, :, :], PR[:, :, :], sm[1].unsqueeze(2).broadcast_to([P, B, E]), ALU.mult)

            def fill(buffer, k, weight):
                link(V.tensor_copy(buffer[:, :, D].bitcast(I32), ROWS[:, k * B:(k + 1) * B]))
                link(V.tensor_copy(buffer[:, :, D + 1], weight))

            def route_by_experts():
                thr, cand, bit, step = (IV[:, k, :] for k in range(4))
                link(V.memset(thr, 0))
                link(V.memset(cand, 1 << TOP_BIT))
                link(V.memset(bit, 1 << (TOP_BIT - 1)))
                link(V.memset(BITF[:, :], float(1 << TOP_BIT)))
                base = chain.before + chain.n
                LINKS = 6
                with dve.Fori(0, TOP_BIT + 1) as t:
                    chain.before, chain.n = base + t * LINKS, 0
                    tt(ra, pr, over_b(cand.bitcast(F32)), ALU.is_ge)
                    V.tensor_reduce(out=CN[:, :], in_=ra, op=ALU.add, axis=AX_X).then_inc(mask_ready, 1)
                    dve.wait_ge(counted, t + 1)
                    ts(step, PO[:, 0:E], float(CAP), ALU.is_ge, BITF[:, :], ALU.mult)
                    tt(thr, thr, step, ALU.bitwise_or)
                    tt(cand, thr, bit, ALU.bitwise_or)
                    ts(bit, bit, 1, ALU.logical_shift_right)
                    ts(BITF[:, :], BITF[:, :], 0.5, ALU.mult)
                    assert chain.n == LINKS
                chain.before, chain.n = base + (TOP_BIT + 1) * LINKS, 0
                thr = thr.bitcast(F32)
                tt(ra, pr, over_b(thr), ALU.is_gt)
                tt(oh, pr, over_b(thr), ALU.is_equal)
                link(V.tensor_copy(MASK[:, :, :], oh))
                V.tensor_reduce(out=CN[:, :], in_=ra, op=ALU.add, axis=AX_X).then_inc(mask_ready, 1)
                ranks(1)
                ts(ex[0], PO[:, 0:E], -1.0, ALU.mult, float(CAP), ALU.add)
                tt(rk, rk, over_b(ex[0]), ALU.is_lt)
                tt(oh, oh, rk, ALU.mult)
                tt(ra, ra, oh, ALU.add)
                reduce(sm[2], by_row(ra), ALU.max)
                ts(sm[2], sm[2], -1.0, ALU.mult, 1.0, ALU.add)
                tt(rb, ra, over_e(sm[2]), ALU.max)
                tt(rk, pr, rb, ALU.mult)
                ts(rb, rb, -1.0, ALU.add)
                tt(rk, rk, rb, ALU.add)
                first_best(rk, sm[3], oh)
                V.tensor_copy(MASK[:, :, :], oh).then_inc(mask_ready, 1)
                ranks(2)
                tt(rk, rk, over_b(const("expert_region")), ALU.add)
                slot_of(oh, 0)
                fill(N, 0, sm[3])

            def route_by_tokens():
                first_best(pr, sm[3], oh)
                ts(rk, oh, -2.0, ALU.mult)
                tt(rk, rk, pr, ALU.add)
                first_best(rk, sm[4], ra)
                V.tensor_tensor(out=MASK[:, :, :], in0=oh, in1=ra, op=ALU.add).then_inc(mask_ready, 1)
                tt(sm[5], sm[3], sm[4], ALU.add)
                ts(sm[5], sm[5], 1e-9, ALU.add)
                link(V.reciprocal(sm[5], sm[5]))
                tt(sm[3], sm[3], sm[5], ALU.mult)
                tt(sm[4], sm[4], sm[5], ALU.mult)
                ranks(3)
                tt(rk, rk, over_b(const("expert_region")), ALU.add)
                slot_of(oh, 0)
                slot_of(ra, 1)
                fill(N, 0, sm[3])
                fill(N2, 1, sm[4])

            def expert_layer(layer):
                probabilities(layer)
                dve.wait_ge(n_copied, PAIRS * (layer + 1))
                (route_by_experts, route_by_tokens)[layer]()
                link(V.tensor_copy(ex[6], ex[1]))
                V.tensor_copy(ex[7], ex[6]).then_inc(copied, 1)
                tables(layer)
                W, hid = WCOLS[layer], HID[layer]
                if layer == 1:
                    dve.wait_ge(w_loaded, 16)

                def slot(tile):
                    if a := tile(-1):
                        dve.wait_ge(y_done, a.g + 1)
                        dve.wait_ge(meta, a.g + 1)
                        dve.wait_ge(w_kept, a.g + 1)
                        old = (a.r + 2) % 4
                        dve.wait_ge(SC[old], 32 * a.n if a.r < 2 else 32 * (a.n + 1))
                        y = bank[6 + a.u][:, 0:2 * D].rearrange("p (c d) -> p c d", c=2)
                        if layer == 1:
                            link(V.tensor_tensor(out=YS[:, a.u, :, :], in0=y,
                                                 in1=WR[:, a.u, W - D:W].unsqueeze(1).broadcast_to([P, 2, D]), op=ALU.add))
                            y = YS[:, a.u, :, :]
                        for c in range(2):
                            last = V.tensor_scalar(out=YS[:, a.u, c, :], in0=y[:, c], scalar1=META_W[:, a.r, c:c + 1],
                                                   scalar2=None, op0=ALU.mult)
                        last.then_inc(y_kept, 1)
                    if a := tile(1):
                        dve.wait_ge(y_done, before(a.g - 1))
                        dve.wait_ge(y_kept, before(a.g - 1))
                        r = dve.value_load(TBL[0:1, 1, bass.ds(a.i, 1)], min_val=0, max_val=(E - 1) * W)
                        V.tensor_copy(WR[:, a.u, 0:W], WALL[:, bass.ds(r, W)]).then_inc(w_kept, 1)
                        dve.wait_ge(XGS[a.u], 16 * (a.h + 1))
                        dve.wait_ge(SC[a.r], 32 * a.n)
                        V.tensor_copy(META_ROW[:, a.r, :], XG[:, a.u, :, D].bitcast(I32))
                        V.tensor_copy(META_W[:, a.r, :], XG[:, a.u, :, D + 1]).then_inc(meta, 1)

                tile_slots(dve, layer, slot, chain, layer)
                dve.wait_ge(y_loaded, 16 * (1, 3)[layer])
                CH = B // 4
                for k in range(4):
                    rows = slice(k * CH, (k + 1) * CH)
                    x = X[:, k * CH * D:(k + 1) * CH * D].rearrange("p (b d) -> p b d", b=CH)
                    if layer == 1:
                        link(V.tensor_tensor(out=N2[:, rows, 0:D], in0=N2[:, rows, 0:D], in1=N[:, rows, 0:D], op=ALU.add))
                    link(V.scalar_tensor_tensor(out=x, in0=N2[:, rows, 0:D], scalar=GATES[:, 2 + layer:3 + layer], in1=x,
                                                op0=ALU.mult, op1=ALU.add))
                V.tensor_copy(ex[7], ex[6]).then_inc(combined, 1)

            for layer in range(2):
                pair_slots(dve, layer, attention_slot(layer), chain, (6, 5)[layer])
                expert_layer(layer)


def kernel(x, ctx_1024, g_xattn, g_ffn, L0_xattn_Wq, L0_xattn_bq, L0_xattn_Wk, L0_xattn_bk, L0_xattn_Wv, L0_xattn_bv,
           L0_xattn_Wo, L0_xattn_bo, L0_ffn_Wg, L0_ffn_W1, L0_ffn_W2, L1_xattn_Wq, L1_xattn_Wkv, L1_ffn_gate_w, L1_ffn_w1,
           L1_ffn_b1, L1_ffn_w2, L1_ffn_b2):
    import concourse.bacc as bacc
    from concourse.bass_utils import run_bass_kernel_spmd

    f = lambda a: np.ascontiguousarray(a)
    over = lambda v: np.broadcast_to(np.asarray(v)[None, :], (P, v.shape[0]))
    at, const, sel, rows, pads = constants()
    Wkv = np.asarray(L1_xattn_Wkv)
    squares = [np.asarray(w).T for w in (L0_xattn_Wq, L0_xattn_Wk, L0_xattn_Wv, L0_xattn_Wo)]
    squares += [np.asarray(L1_xattn_Wq), Wkv[:, 0:D], Wkv[:, D:2 * D]]

    def experts(w1, w2):
        e, _, hid = w1.shape
        return [np.transpose(np.asarray(w1), (1, 0, 2)),
                np.transpose(np.asarray(w2).reshape(e, hid // P, P, D), (2, 0, 1, 3)).reshape(P, e, hid // P * D)]

    zero = np.zeros((P, 2), np.float32)
    b1 = np.transpose(np.asarray(L1_ffn_b1).reshape(E, HID[1] // P, P), (2, 0, 1))
    b2 = np.broadcast_to(np.asarray(L1_ffn_b2)[None], (P, E, D))
    arrays = {
        "x": f(x), "ctx": f(ctx_1024),
        "gates": f(np.concatenate([over(g_xattn), over(g_ffn)], axis=1)),
        "wsq": f(np.stack(squares, axis=1)),
        "wg": f(np.stack([np.asarray(L0_ffn_Wg), np.asarray(L1_ffn_gate_w).T], axis=1)),
        "vec": f(np.concatenate([over(L0_xattn_bv), over(L0_xattn_bo), np.asarray(L0_xattn_bq)[:, None],
                                 np.asarray(L0_xattn_bk)[:, None], zero], axis=1)),
        "w0": f(np.concatenate(experts(L0_ffn_W1, L0_ffn_W2), axis=2).reshape(P, -1)),
        "w1": f(np.concatenate(experts(L1_ffn_w1, L1_ffn_w2) + [b1, b2], axis=2).reshape(P, -1)),
        "const": f(const), "sel": f(sel), "rows": f(rows), "pads": f(pads),
    }
    nc = bacc.Bacc("TRN2", target_bir_lowering=False, num_devices=1)
    args = [nc.dram_tensor(f"in_{n}", a.shape, mybir.dt.from_np(a.dtype), kind="ExternalInput").ap() for n, a in arrays.items()]
    out = nc.dram_tensor("out", (B, P, D), F32, kind="ExternalOutput").ap()
    program(nc, at, *args, out)
    result = run_bass_kernel_spmd(nc, [{f"in_{n}": a for n, a in arrays.items()}], core_ids=[0])
    return result.results[0]["out"]
```
